# Optimizing a Trainium2 kernel written in Bass

```python
import numpy as np
import jax
import jax.numpy as jnp

def _softmax(x, axis=-1):
    return jax.nn.softmax(x, axis=axis)

def _gelu(x):
    return jax.nn.gelu(x, approximate=True)

def _silu(x):
    return jax.nn.silu(x)

def _sigmoid(x):
    return jax.nn.sigmoid(x)

def _layernorm(x, axis=-1, eps=1e-05):
    m = jnp.mean(x, axis=axis, keepdims=True)
    v = jnp.var(x, axis=axis, keepdims=True)
    return (x - m) / jnp.sqrt(v + eps)

def _scatter_add(tgt, idx, src, axis=0):
    return tgt.at[idx].add(src)

def _segment_sum(src, seg, n):
    return jax.ops.segment_sum(src, seg, n)
kernel_name = 'mk_gnn_preln_d4_gnn_r8_484713'

def setup_inputs(seed: int=0):
    np.random.seed(seed)
    _w = jnp.asarray

    def _rec_inputs():
        import jax
        import jax.numpy as jnp
        _gk = jax.random.key(seed)
        x = 0.0001712 + 1 * jax.random.normal(jax.random.fold_in(_gk, 1), (12500, 16), jnp.float32)
        src = jax.random.randint(jax.random.fold_in(_gk, 2), (400000,), 0, 12500, jnp.int32)
        dst = jnp.minimum((12500 * jax.random.uniform(jax.random.fold_in(_gk, 3), (400000,)) ** 2.0).astype(jnp.int32), 99999)
        _o = jnp.argsort(dst, stable=True)
        src = src[_o]
        dst = dst[_o]
        edge_attr_13 = 2.91757e-06 + 0.999892 * jax.random.normal(jax.random.fold_in(_gk, 12), (400000, 13), jnp.float32)
        edge_attr_8 = -5.3897e-05 + 0.999841 * jax.random.normal(jax.random.fold_in(_gk, 13), (400000, 8), jnp.float32)
        edge_type_8 = jax.random.randint(jax.random.fold_in(_gk, 15), (400000,), 0, 8, jnp.int32)
        edge_weight = jax.random.uniform(jax.random.fold_in(_gk, 16), (400000,), jnp.float32, 0.0, 1)
        node_vec1 = -0.00472126 + 0.997171 * jax.random.normal(jax.random.fold_in(_gk, 17), (12500, 1), jnp.float32)
        return (x, src, dst, edge_attr_13, edge_attr_8, edge_type_8, edge_weight, node_vec1)
    x, src, dst, edge_attr_13, edge_attr_8, edge_type_8, edge_weight, node_vec1 = _rec_inputs()

    def _L0_gnn_setup():
        import jax, jax.numpy as jnp
        import numpy as np
        N = 6250
        E = 100000
        NC = 16
        FDIM = 13
        HID = 32
        NREPEATS = 2

        def _gru_cell(x, h, w_ih, w_hh, b_ih, b_hh):
            gi = x @ w_ih.T + b_ih
            gh = h @ w_hh.T + b_hh
            i_r, i_z, i_n = jnp.split(gi, 3, axis=1)
            h_r, h_z, h_n = jnp.split(gh, 3, axis=1)
            r = jax.nn.sigmoid(i_r + h_r)
            z = jax.nn.sigmoid(i_z + h_z)
            n = jnp.tanh(i_n + r * h_n)
            return (1.0 - z) * n + z * h
        key = jax.random.key(seed)
        ks = jax.random.split(key, 10)
        hx = jax.random.normal(ks[0], (N, NC), dtype=jnp.float32)
        edgefeats = jax.random.normal(ks[1], (E, FDIM), dtype=jnp.float32)
        edge_src = jax.random.randint(ks[2], (E,), 0, N, dtype=jnp.int32)
        edge_dst = jax.random.randint(ks[3], (E,), 0, N, dtype=jnp.int32)
        fnet_w1 = jax.random.normal(ks[4], (FDIM, HID), dtype=jnp.float32) * (1.0 / np.sqrt(FDIM))
        fnet_b1 = jnp.zeros((HID,), dtype=jnp.float32)
        fnet_w2 = jax.random.normal(ks[5], (HID, NC * NC), dtype=jnp.float32) * (0.1 / np.sqrt(HID))
        fnet_b2 = jnp.zeros((NC * NC,), dtype=jnp.float32)
        gru_w_ih = jax.random.normal(ks[6], (3 * NC, NC), dtype=jnp.float32) * (1.0 / np.sqrt(NC))
        gru_w_hh = jax.random.normal(ks[7], (3 * NC, NC), dtype=jnp.float32) * (1.0 / np.sqrt(NC))
        gru_b_ih = jnp.zeros((3 * NC,), dtype=jnp.float32)
        gru_b_hh = jnp.zeros((3 * NC,), dtype=jnp.float32)
        return {'hx': hx, 'edgefeats': edgefeats, 'edge_src': edge_src, 'edge_dst': edge_dst, 'fnet_w1': fnet_w1, 'fnet_b1': fnet_b1, 'fnet_w2': fnet_w2, 'fnet_b2': fnet_b2, 'gru_w_ih': gru_w_ih, 'gru_w_hh': gru_w_hh, 'gru_b_ih': gru_b_ih, 'gru_b_hh': gru_b_hh}
    _L0_gnn_all = _L0_gnn_setup()
    _L0_gnn_in = {k: v for k, v in _L0_gnn_all.items() if k in ('fnet_w1', 'fnet_b1', 'fnet_w2', 'fnet_b2', 'gru_w_ih', 'gru_w_hh', 'gru_b_ih', 'gru_b_hh')}
    del _L0_gnn_all

    def _L1_gnn_setup():
        import jax, jax.numpy as jnp
        import numpy as np
        N_NODES = 12500
        N_EDGES = 400000
        D_NODE = 16
        D_EDGE = 8
        D_HIDDEN = 16
        key = jax.random.key(seed)
        ks = jax.random.split(key, 8)
        node_features = jax.random.normal(ks[0], (N_NODES, D_NODE), dtype=jnp.float32)
        edge_attr_e3nn = jax.random.normal(ks[1], (N_EDGES, D_EDGE), dtype=jnp.float32)
        node_attr_scalar_raw = jax.random.normal(ks[2], (N_NODES, 1), dtype=jnp.float32)
        W_msg_tp = jax.random.normal(ks[3], (D_NODE, D_EDGE, D_HIDDEN), dtype=jnp.float32)
        W_msg_lin = jax.random.normal(ks[4], (D_HIDDEN, D_HIDDEN), dtype=jnp.float32)
        W_upd_tp = jax.random.normal(ks[5], (D_NODE, D_HIDDEN, D_HIDDEN), dtype=jnp.float32)
        W_upd_lin = jax.random.normal(ks[6], (D_HIDDEN, D_NODE), dtype=jnp.float32)
        edge_index = jax.random.randint(ks[7], (2, N_EDGES), 0, N_NODES, dtype=jnp.int64)
        return {'node_features': node_features, 'edge_attr_e3nn': edge_attr_e3nn, 'node_attr_scalar_raw': node_attr_scalar_raw, 'W_msg_tp': W_msg_tp, 'W_msg_lin': W_msg_lin, 'W_upd_tp': W_upd_tp, 'W_upd_lin': W_upd_lin, 'edge_index': edge_index}
    _L1_gnn_all = _L1_gnn_setup()
    _L1_gnn_in = {k: v for k, v in _L1_gnn_all.items() if k in ('W_msg_tp', 'W_msg_lin', 'W_upd_tp', 'W_upd_lin')}
    del _L1_gnn_all

    def _L2_gnn_setup():
        import jax, jax.numpy as jnp
        import numpy as np
        N_NODES = 12500
        N_EDGES = 400000
        NUM_REL = 8

        def _rgcn_layer(x, src, dst, edge_type, W, root, bias):
            out = x @ root + bias
            x_src = x[src]
            for r in range(W.shape[0]):
                mask = (edge_type == r).astype(x.dtype)
                s = jax.ops.segment_sum(x_src * mask[:, None], dst, num_segments=x.shape[0])
                cnt = jax.ops.segment_sum(mask, dst, num_segments=x.shape[0])
                agg = s / jnp.clip(cnt, 1.0)[:, None]
                out = out + agg @ W[r]
            return out
        key = jax.random.key(seed)
        ks = jax.random.split(key, 9)
        x = jax.random.normal(ks[0], (N_NODES, 16), dtype=jnp.float32)
        edge_index = jax.random.randint(ks[1], (2, N_EDGES), 0, N_NODES, dtype=jnp.int32)
        edge_type = jax.random.randint(ks[2], (N_EDGES,), 0, NUM_REL, dtype=jnp.int32)
        s1 = 1.0 / np.sqrt(16.0)
        s2 = 1.0 / np.sqrt(32.0)
        W1 = jax.random.normal(ks[3], (NUM_REL, 16, 32), dtype=jnp.float32) * s1
        root1 = jax.random.normal(ks[4], (16, 32), dtype=jnp.float32) * s1
        b1 = jnp.zeros((32,), dtype=jnp.float32)
        W2 = jax.random.normal(ks[5], (NUM_REL, 32, 16), dtype=jnp.float32) * s2
        root2 = jax.random.normal(ks[6], (32, 16), dtype=jnp.float32) * s2
        b2 = jnp.zeros((16,), dtype=jnp.float32)
        return {'x': x, 'edge_index': edge_index, 'edge_type': edge_type, 'W1': W1, 'root1': root1, 'b1': b1, 'W2': W2, 'root2': root2, 'b2': b2}
    _L2_gnn_all = _L2_gnn_setup()
    _L2_gnn_in = {k: v for k, v in _L2_gnn_all.items() if k in ('W1', 'root1', 'b1', 'W2', 'root2', 'b2')}
    del _L2_gnn_all

    def _L3_gnn_setup():
        import jax, jax.numpy as jnp
        import numpy as np
        N_NODES = 12500
        N_EDGES = 400000
        DIM = 16
        B, K, C, D, E, H = (0.1, 5.0, 1.0, 5.0, 0.9, 0.1)
        E_ = E
        key = jax.random.key(seed)
        k1, k2, k3, k4 = jax.random.split(key, 4)
        x = jax.random.uniform(k1, (N_NODES, DIM), dtype=jnp.float32)
        edge_src = jax.random.randint(k2, (N_EDGES,), 0, N_NODES, dtype=jnp.int32)
        edge_dst = jax.random.randint(k3, (N_EDGES,), 0, N_NODES, dtype=jnp.int32)
        edge_vals = jax.random.uniform(k4, (N_EDGES,), dtype=jnp.float32)
        return {'x': x, 'edge_src': edge_src, 'edge_dst': edge_dst, 'edge_vals': edge_vals}
    _L3_gnn_all = _L3_gnn_setup()
    _L3_gnn_in = {k: v for k, v in _L3_gnn_all.items() if k in ()}
    del _L3_gnn_all
    return {'x': x, 'src': src, 'dst': dst, 'edge_attr_13': edge_attr_13, 'edge_attr_8': edge_attr_8, 'edge_type_8': edge_type_8, 'edge_weight': edge_weight, 'node_vec1': node_vec1, 'L0_gnn_fnet_w1': _L0_gnn_in['fnet_w1'], 'L0_gnn_fnet_b1': _L0_gnn_in['fnet_b1'], 'L0_gnn_fnet_w2': _L0_gnn_in['fnet_w2'], 'L0_gnn_fnet_b2': _L0_gnn_in['fnet_b2'], 'L0_gnn_gru_w_ih': _L0_gnn_in['gru_w_ih'], 'L0_gnn_gru_w_hh': _L0_gnn_in['gru_w_hh'], 'L0_gnn_gru_b_ih': _L0_gnn_in['gru_b_ih'], 'L0_gnn_gru_b_hh': _L0_gnn_in['gru_b_hh'], 'L1_gnn_W_msg_tp': _L1_gnn_in['W_msg_tp'], 'L1_gnn_W_msg_lin': _L1_gnn_in['W_msg_lin'], 'L1_gnn_W_upd_tp': _L1_gnn_in['W_upd_tp'], 'L1_gnn_W_upd_lin': _L1_gnn_in['W_upd_lin'], 'L2_gnn_W1': _L2_gnn_in['W1'], 'L2_gnn_root1': _L2_gnn_in['root1'], 'L2_gnn_b1': _L2_gnn_in['b1'], 'L2_gnn_W2': _L2_gnn_in['W2'], 'L2_gnn_root2': _L2_gnn_in['root2'], 'L2_gnn_b2': _L2_gnn_in['b2']}

def reference(x, src, dst, edge_attr_13, edge_attr_8, edge_type_8, edge_weight, node_vec1, L0_gnn_fnet_w1, L0_gnn_fnet_b1, L0_gnn_fnet_w2, L0_gnn_fnet_b2, L0_gnn_gru_w_ih, L0_gnn_gru_w_hh, L0_gnn_gru_b_ih, L0_gnn_gru_b_hh, L1_gnn_W_msg_tp, L1_gnn_W_msg_lin, L1_gnn_W_upd_tp, L1_gnn_W_upd_lin, L2_gnn_W1, L2_gnn_root1, L2_gnn_b1, L2_gnn_W2, L2_gnn_root2, L2_gnn_b2):
    import jax
    import jax.numpy as jnp

    def _L0_gnn_ref(hx, edgefeats, edge_src, edge_dst, fnet_w1, fnet_b1, fnet_w2, fnet_b2, gru_w_ih, gru_w_hh, gru_b_ih, gru_b_hh):
        import jax, jax.numpy as jnp
        import numpy as np
        N = 6250
        E = 100000
        NC = 16
        FDIM = 13
        HID = 32
        NREPEATS = 2

        def _gru_cell(x, h, w_ih, w_hh, b_ih, b_hh):
            gi = x @ w_ih.T + b_ih
            gh = h @ w_hh.T + b_hh
            i_r, i_z, i_n = jnp.split(gi, 3, axis=1)
            h_r, h_z, h_n = jnp.split(gh, 3, axis=1)
            r = jax.nn.sigmoid(i_r + h_r)
            z = jax.nn.sigmoid(i_z + h_z)
            n = jnp.tanh(i_n + r * h_n)
            return (1.0 - z) * n + z * h
        n_nodes, nc = hx.shape
        w = jax.nn.relu(edgefeats @ fnet_w1 + fnet_b1) @ fnet_w2 + fnet_b2
        W = w.reshape(-1, nc, nc)
        deg = jax.ops.segment_sum(jnp.ones((edge_dst.shape[0],), hx.dtype), edge_dst, num_segments=n_nodes)
        inv_deg = 1.0 / jnp.maximum(deg, 1.0)
        for _ in range(NREPEATS):
            xj = hx[edge_src]
            m = jnp.einsum('ei,eio->eo', xj, W)
            agg = jax.ops.segment_sum(m, edge_dst, num_segments=n_nodes)
            agg = agg * inv_deg[:, None]
            hx = _gru_cell(agg, hx, gru_w_ih, gru_w_hh, gru_b_ih, gru_b_hh)
        return hx

    def _L1_gnn_ref(node_features, edge_attr_e3nn, node_attr_scalar_raw, W_msg_tp, W_msg_lin, W_upd_tp, W_upd_lin, edge_index):
        import jax, jax.numpy as jnp
        import numpy as np
        N_NODES = 12500
        N_EDGES = 400000
        D_NODE = 16
        D_EDGE = 8
        D_HIDDEN = 16
        n_nodes = node_features.shape[0]
        row = edge_index[0]
        col = edge_index[1]
        norm_msg_tp = 1.0 / np.float32(np.sqrt(D_NODE * D_EDGE))
        norm_upd_tp = 1.0 / np.float32(np.sqrt(D_NODE * D_HIDDEN))
        norm_lin = 1.0 / np.float32(np.sqrt(D_HIDDEN))
        x_j = node_features[col]
        m = jnp.einsum('ei,ej,ijh->eh', x_j, edge_attr_e3nn, W_msg_tp) * norm_msg_tp
        m = jax.nn.silu(m)
        m = m @ W_msg_lin * norm_lin
        agg = jax.ops.segment_sum(m, row, num_segments=n_nodes)
        u = jnp.einsum('ni,nh,ihk->nk', node_features, agg, W_upd_tp) * norm_upd_tp
        u = jax.nn.silu(u)
        u = u @ W_upd_lin * norm_lin
        return node_features + u

    def _L2_gnn_ref(x, edge_index, edge_type, W1, root1, b1, W2, root2, b2):
        import jax, jax.numpy as jnp
        import numpy as np
        N_NODES = 12500
        N_EDGES = 400000
        NUM_REL = 8

        def _rgcn_layer(x, src, dst, edge_type, W, root, bias):
            out = x @ root + bias
            x_src = x[src]
            for r in range(W.shape[0]):
                mask = (edge_type == r).astype(x.dtype)
                s = jax.ops.segment_sum(x_src * mask[:, None], dst, num_segments=x.shape[0])
                cnt = jax.ops.segment_sum(mask, dst, num_segments=x.shape[0])
                agg = s / jnp.clip(cnt, 1.0)[:, None]
                out = out + agg @ W[r]
            return out
        src, dst = (edge_index[0], edge_index[1])
        h = _rgcn_layer(x, src, dst, edge_type, W1, root1, b1)
        h = jax.nn.relu(h)
        h = _rgcn_layer(h, src, dst, edge_type, W2, root2, b2)
        return h

    def _L3_gnn_ref(x, edge_src, edge_dst, edge_vals):
        import jax, jax.numpy as jnp
        import numpy as np
        N_NODES = 12500
        N_EDGES = 400000
        DIM = 16
        B, K, C, D, E, H = (0.1, 5.0, 1.0, 5.0, 0.9, 0.1)
        E_ = E
        n = x.shape[0]
        f = B + x * (1.0 - x / K) * (x / C - 1.0)
        xi = x[edge_src]
        xj = x[edge_dst]
        msg = edge_vals[:, None] * xi * xj / (D + E_ * xi + H * xj)
        f = f + jax.ops.segment_sum(msg, edge_src, num_segments=n)
        return f
    edge_index = jnp.stack([src, dst])
    h = jnp.maximum(_layernorm(x, axis=-1), 0.0)
    x = x + _L0_gnn_ref(h, edge_attr_13, src, dst, L0_gnn_fnet_w1, L0_gnn_fnet_b1, L0_gnn_fnet_w2, L0_gnn_fnet_b2, L0_gnn_gru_w_ih, L0_gnn_gru_w_hh, L0_gnn_gru_b_ih, L0_gnn_gru_b_hh)
    h = jnp.maximum(_layernorm(x, axis=-1), 0.0)
    x = x + _L1_gnn_ref(h, edge_attr_8, node_vec1, L1_gnn_W_msg_tp, L1_gnn_W_msg_lin, L1_gnn_W_upd_tp, L1_gnn_W_upd_lin, edge_index)
    h = jnp.maximum(_layernorm(x, axis=-1), 0.0)
    x = x + _L2_gnn_ref(h, edge_index, edge_type_8, L2_gnn_W1, L2_gnn_root1, L2_gnn_b1, L2_gnn_W2, L2_gnn_root2, L2_gnn_b2)
    h = jnp.maximum(_layernorm(x, axis=-1), 0.0)
    x = x + _L3_gnn_ref(h, src, dst, edge_weight)
    return x

_drawn_inputs = setup_inputs


def setup_inputs(seed=0):
    import zlib

    import numpy as np

    out = dict(_drawn_inputs(seed))
    spreads = {'L0_gnn_fnet_b1': (0.0, 0.8),
     'L0_gnn_fnet_b2': (0.0, 0.1),
     'L0_gnn_gru_b_ih': (0.0, 0.1),
     'L0_gnn_gru_b_hh': (0.0, 0.1),
     'L2_gnn_b1': (0.0, 0.1),
     'L2_gnn_b2': (0.0, 0.271)}
    factors = {'edge_attr_13': 4.13, 'L0_gnn_fnet_w1': 3.528, 'L0_gnn_fnet_w2': 2.791}
    for name, (base, spread) in spreads.items():
        noise = np.random.default_rng([zlib.crc32(name.encode()), seed]).standard_normal(out[name].shape)
        drawn = base * np.exp(spread * noise) if base else spread * noise
        out[name] = jnp.asarray(drawn.astype(out[name].dtype))
    for name, factor in factors.items():
        out[name] = (out[name] * factor).astype(out[name].dtype)
    return out
```

```python
import concourse.bass as bass
from concourse import mybir
from contextlib import ExitStack

F32 = mybir.dt.float32
I32 = mybir.dt.int32
BF16 = mybir.dt.bfloat16
ALU = mybir.AluOpType
ACT = mybir.ActivationFunctionType
AX = mybir.AxisListType

P = 128
N_NODES = 12500
N_EDGES = 400000
D = 16
BUCKETS = -(-N_NODES // P)
N_PAD = BUCKETS * P
LAST = N_NODES - (BUCKETS - 1) * P

TILES_GROUP = 2
GROUP = TILES_GROUP * P
GROUPS_BLOCK = 2
T = TILES_GROUP * GROUPS_BLOCK
BLOCK = T * P
SLOTS = 4
MAX_GROUPS = (N_EDGES + BUCKETS * (GROUP - 1)) // GROUP
ITERS = -(-MAX_GROUPS // (GROUPS_BLOCK * SLOTS))
ITERS += -ITERS % 4
BLOCKS = ITERS * SLOTS
GROUPS = BLOCKS * GROUPS_BLOCK
ATTR_D = 13
PARTS = 3
ATTR_W = PARTS * ATTR_D + 1
REC = {"dst": 24, "src": 16}
C_LANE, C_OTHER, C_LAST = ({"dst": 20 + n, "src": 8 + n} for n in range(3))
PAD_LANE = 255.0

J = 25
CHUNK = P * J
CHUNKS = N_EDGES // CHUNK

HID = 32
HID_W = PARTS * HID + 1
RELS = 8
EDGE_D = 8
W2A = RELS * D + RELS
NODE_TILES = 7
NODE_STEPS = BUCKETS // NODE_TILES
PAD_ROWS = 64
LN_EPS = 1e-5
NORM_MSG = float((D * EDGE_D) ** -0.5)
NORM_UPD = float((D * D) ** -0.5)
NORM_LIN = float(D ** -0.5)

PAD_DMAS = BLOCKS * BLOCK // (P * PAD_ROWS)

L0A, L0B, L1, L2A, L2B, L3 = range(6)
BY_DST = (L0A, L0B, L2A, L2B)
TABLE_W = {L0A: D, L0B: D, L1: D * EDGE_D, L2A: D, L2B: D, L3: D}
(N_GRU0, N_GRU1, N_Y, N_UPD, N_UPD2, N_ROOT1, N_REL1, N_Z, N_ROOT2) = range(9)


def gnn_kernel(nc, a, out):
    ctx = ExitStack()
    with ctx:
        def sb(name, shape, dt=F32):
            return ctx.enter_context(nc.sbuf_tensor(name, shape, dt))

        def sem(name):
            return ctx.enter_context(nc.semaphore(name))

        def dram(name, shape, dt=F32):
            return nc.dram_tensor(name, shape, dt, kind="Internal").ap()

        bucket_rows = {"dst": dram("bucket_dst", (N_EDGES,), BF16), "src": dram("bucket_src", (N_EDGES,), BF16)}
        recs = {k: dram(f"rec_{k}", (BLOCKS * BLOCK, REC[k])) for k in ("dst", "src")}
        tables = {p: dram(f"table{p}", (N_PAD, TABLE_W[p])) for p in (L0A, L0B, L1, L2A, L3)}
        tables[L2B] = dram("table_rel", (N_PAD * RELS, D))

        x_n = sb("x_n", [P, BUCKETS, D])
        h_n = sb("h_n", [P, BUCKETS, D])
        t_n = sb("t_n", [P, BUCKETS, D])
        u_n = sb("u_n", [P, BUCKETS, D])
        stat = sb("stat", [P, 3, BUCKETS])
        inv = sb("inv", [P, BUCKETS, RELS])
        agg17 = sb("agg17", [P, BUCKETS, D + 1])
        agg16 = agg17[:, :, 0:D]
        big = sb("big", [P, BUCKETS, W2A])
        wide = big[:, :, 0:P]
        SORT_WORDS = 2 * CHUNK // 2 + CHUNK // 2 + CHUNK + 2 * CHUNK
        NODE_WORDS = BUCKETS * (2 * HID) + BUCKETS * (2 * D + 2)
        shared = sb("shared", [P, max(SORT_WORDS, NODE_WORDS)])
        o = 0
        hi_in = []
        for s in range(2):
            hi_in.append(shared[:, o:o + CHUNK // 2].bitcast(BF16))
            o += CHUNK // 2
        eq = shared[:, o:o + CHUNK // 2].bitcast(BF16)
        o += CHUNK // 2
        cum = shared[:, o:o + CHUNK]
        o += CHUNK
        picked = [shared[:, o + s * CHUNK:o + (s + 1) * CHUNK] for s in range(2)]
        gates = shared[:, 0:BUCKETS * 2 * HID].rearrange("p (b f) -> p b f", b=BUCKETS)
        node_in = shared[:, BUCKETS * 2 * HID:NODE_WORDS].rearrange("p (b f) -> p b f", b=BUCKETS)

        idx_all = big[:, :, :].rearrange("p b f -> p (b f)")[:, 0:N_EDGES // P].bitcast(I32)
        hi_int = big[:, :, :].rearrange("p b f -> p (b f)")[:, N_EDGES // P:2 * (N_EDGES // P)].bitcast(I32)
        hi_bf = [shared[:, s * 1600:(s + 1) * 1600].bitcast(BF16) for s in range(2)]
        pad_rec = {k: big[:, :, :].rearrange("p b f -> p (b f)")[:, o:o + PAD_ROWS * REC[k]]
                   for k, o in (("dst", 8192), ("src", 8192 + PAD_ROWS * REC["dst"]))}

        REC_WORDS = 2 * J * REC["dst"]
        rec_room = sb("rec_room", [P, max(REC_WORDS, 2 * BLOCK)])
        rec_out = rec_room[:, 0:REC_WORDS].rearrange("p (s j f) -> p s j f", s=2, j=J)
        onehot_t = rec_room[:, 0:2 * BLOCK].rearrange("p (v e) -> p v e", v=2)
        where = sb("where", [P, 2, J], I32)
        carry = {k: sb(f"carry_{k}", [P, 1]) for k in ("dst", "src")}
        n_groups = {k: sb(f"n_groups_{k}", [P, 1]) for k in ("dst", "src")}
        n_i = sb("n_i", [P, 1], I32)
        end_g = sb("end_g", [P, 1])
        iota_p = sb("iota_p", [P, 1])
        iota_f = sb("iota_f", [P, P])
        upto = sb("upto", [P, P])
        ones = sb("ones", [P, P])
        ident = sb("ident", [P, P])
        ident_bf = sb("ident_bf", [P, P], BF16)
        started = picked[0][:, 0:GROUPS]
        bucket_of = {k: sb(f"bucket_of_{k}", [1, GROUPS], I32) for k in ("dst", "src")}
        iota_g = cum[:, 0:GROUPS]

        rec = {k: sb(f"rec_{k}_in", [P, SLOTS, T, REC[k]]) for k in ("dst", "src")}
        got = sb("got", [P, SLOTS, T, D * EDGE_D])
        onehot = sb("onehot", [P, 2, T, P])
        got_flat = got[:, :, :, :].rearrange("p u t f -> p (u t f)")
        attr_in = got_flat[:, 0:2 * J * ATTR_D].rearrange("p (s f) -> p s f", s=2)
        o = 2 * J * ATTR_D
        key_in, other_in, last_in = (got_flat[:, o + n * 2 * J:o + (n + 1) * 2 * J].bitcast(I32)
                                     .rearrange("p (s j) -> p s j", s=2) for n in range(3))
        o += 3 * 2 * J
        lane_i, pos_i, pos_b, pos_c = (got_flat[:, o + n * J:o + (n + 1) * J].bitcast(I32) for n in range(4))
        counts = got_flat[:, o + 4 * J:o + 4 * J + CHUNKS]
        prod = sb("prod", [P, T, D * D])
        prod_flat = prod[:, :, :].rearrange("p t f -> p (t f)")
        attr_rest = prod_flat[:, 0:J * ATTR_D].rearrange("p (j f) -> p j f", j=J)
        msg = sb("msg", [P, 2, T, D])
        msg_rest = sb("msg_rest", [P, 2, T, D])
        msg_parts = sb("msg_parts", [P, 2, PARTS, T, D + 1], BF16)
        onehot_bf = sb("onehot_bf", [P, SLOTS, T, P], BF16)
        iota_bf = sb("iota_bf", [P, P], BF16)
        msg16 = sb("msg16", [P, 2, T, D])
        msgw = sb("msgw", [P, 2, T, W2A])
        rel_i = sb("rel_i", [P, T], I32)
        attr_t = sb("attr_t", [ATTR_W, 2, BLOCK], BF16)
        hid = sb("hid", [P, 2, T, HID])
        hid_rest = sb("hid_rest", [P, 2, T, HID])
        hid_parts = sb("hid_parts", [P, 2, T, HID_W + 1], BF16)
        hid_t = sb("hid_t", [HID_W, 2, BLOCK], BF16)
        small = sb("small", [P, 4, T, D])

        tile_words = NODE_TILES * P
        stage = shared[:, NODE_WORDS:NODE_WORDS + tile_words].rearrange("p (t f) -> p t f", t=NODE_TILES)
        turned = shared[:, NODE_WORDS + tile_words:NODE_WORDS + 2 * tile_words]
        lin_t = shared[0:D, NODE_WORDS + 2 * tile_words:NODE_WORDS + 3 * tile_words]

        w1 = sb("w1", [ATTR_W, HID])
        w2 = sb("w2", [HID_W, D * D])
        w1_parts = sb("w1_parts", [ATTR_W, PARTS, HID], BF16)
        w2_parts = sb("w2_parts", [HID_W, PARTS, D * D], BF16)
        wg = sb("wg", [2 * D + 2, 4 * D])
        wy = sb("wy", [D, D * EDGE_D])
        wlin = sb("wlin", [D, D])
        wupd = sb("wupd", [D, D * D])
        wupd2 = sb("wupd2", [D, D])
        wroot1 = sb("wroot1", [D + 1, HID])
        wrel1 = sb("wrel1", [P, HID])
        wz = sb("wz", [HID, P])
        wroot2 = sb("wroot2", [HID + 1, D])
        weights = [(w1, "w1"), (w2, "w2"), (wg, "wg"), (wy, "wy"), (wlin, "wlin"), (wupd, "wupd"),
                   (wupd2, "wupd2"), (wroot1, "wroot1"), (wrel1, "wrel1"), (wz, "wz"), (wroot2, "wroot2")]

        BANK = 512
        ps = ctx.enter_context(nc.psum_tensor("ps", [P, 8 * BANK], F32))
        ps_pos = [ps[:, s * BANK:s * BANK + J] for s in range(2)]
        ps_end = ps[:, 2 * BANK:2 * BANK + 1]
        ps_bucket = ps[:, 4 * BANK:8 * BANK]
        ps_turn_bf = ps[:, 0:BLOCK // 2].bitcast(BF16)
        ps_hid = ps[:, BANK:BANK + T * HID].rearrange("p (t f) -> p t f", t=T)
        ps_w = [ps[:, (2 + 2 * v) * BANK:(4 + 2 * v) * BANK].rearrange("p (t f) -> p t f", t=T) for v in range(2)]
        ps_acc = [ps[:, (6 + v) * BANK:(7 + v) * BANK] for v in range(2)]
        ps_oht = ps[:, 0:BLOCK]
        ps_xi = [ps[:, (2 + v) * BANK:(2 + v) * BANK + T * D].rearrange("p (t f) -> p t f", t=T) for v in range(2)]
        ps_turn = ps[:, 0:2 * BANK]
        ps_out = ps[:, 2 * BANK:4 * BANK]
        ps_v = ps[:, 4 * BANK:8 * BANK]

        def acc(v, width):
            return ps_acc[v][:, 0:GROUPS_BLOCK * width].rearrange("p (g f) -> p g f", g=GROUPS_BLOCK)

        consts_pool = sem("consts_pool")
        consts_dve = sem("consts_dve")
        weights_in = sem("weights_in")
        x_in = sem("x_in")
        idx_in = sem("idx_in")
        hi_ready = sem("hi_ready")
        hi_out = sem("hi_out")
        pad_ready = sem("pad_ready")
        pads_out = sem("pads_out")
        count_in = [sem(f"count_in{s}") for s in range(2)]
        counted = [sem(f"counted{s}") for s in range(2)]
        n_groups_ready = sem("n_groups_ready")
        ends_ready = sem("ends_ready")
        started_ready = sem("started_ready")
        bucket_ready = sem("bucket_ready")
        tables_read = sem("tables_read")
        keys_in = [sem(f"keys_in{s}") for s in range(2)]
        hi_used = [sem(f"hi_used{s}") for s in range(2)]
        picked_ready = [sem(f"picked_ready{s}") for s in range(2)]
        pos_ready = [sem(f"pos_ready{s}") for s in range(2)]
        where_ready = [sem(f"where_ready{s}") for s in range(2)]
        attr_copied = [sem(f"attr_copied{s}") for s in range(2)]
        records_out = [sem(f"records_out{s}") for s in range(2)]

        class Slots:

            def __init__(self, name, passes, unit=1, credit=0):
                self.sems = [sem(f"{name}{u}") for u in range(SLOTS)]
                self.passes, self.unit, self.credit = list(passes), unit, credit

            def of(self, u):
                return self.sems[u]

            def done(self, p, it, u, back=0):
                turns = it + (u - back) // SLOTS + 1 + self.passes.index(p) * ITERS
                return self.sems[(u - back) % SLOTS], turns * self.unit + self.credit

        ALL = [L0A, L0B, L1, L2A, L2B, L3]
        rec_in = Slots("rec_in", ALL, 16)
        early, late = Slots("gathered", ALL[:4], 16 * T), Slots("gathered_late", ALL[4:], 16 * T)
        gathered = {p: early if p in early.passes else late for p in ALL}
        read = Slots("read", ALL, 1, 1)
        scattered = Slots("scattered", ALL, 1, 1)
        added = Slots("added", ALL, 1, 1)
        attr_turned = Slots("attr_turned", (L0A, L0B))
        attr_ready = Slots("attr_ready", (L0A, L0B))
        hid_done = Slots("hid_done", (L0A, L0B))
        relu_ready = Slots("relu_ready", (L0A, L0B))
        rest_ready = Slots("rest_ready", (L0A, L0B))
        mid_ready = Slots("mid_ready", (L0A, L0B))
        msg_split = Slots("msg_split", (L0A, L0B))
        parts_ready = Slots("parts_ready", (L0A, L0B))
        hid_turned = Slots("hid_turned", (L0A, L0B))
        hid_ready = Slots("hid_ready", (L0A, L0B))
        w_done = Slots("w_done", (L0A, L0B))
        silu_ready = Slots("silu_ready", (L1,), 1, 1)
        oh_ready = Slots("oh_ready", (L3,))
        oh_turned = Slots("oh_turned", (L3,))
        oht_ready = Slots("oht_ready", (L3,))
        xi_done = Slots("xi_done", (L3,))

        pass_open = sem("pass_open")
        table_ready = sem("table_ready")
        table_out = sem("table_out")
        node_src = sem("node_src")
        staged = sem("staged")
        node_turned = sem("node_turned")
        turned_ready = sem("turned_ready")
        lin_done = sem("lin_done")
        lin_ready = sem("lin_ready")
        node_out = sem("node_out")
        node_used = sem("node_used")
        to_act = sem("to_act")
        from_act = sem("from_act")
        out_ready = sem("out_ready")
        out_done = sem("out_done")

        COUNT_TURNS = {"dst": 0, "src": 1}

        def chunk_turns(k, c2, s):
            return COUNT_TURNS[k] * ((CHUNKS + 1 - s) // 2) + c2 + 1

        def chunk_loop(eng, body):
            for s in range(2):
                body(0, s)
            with eng.Fori(1, CHUNKS // 2) as c2:
                for s in range(2):
                    body(c2, s)
            body(CHUNKS // 2, 0)

        def block_loop(eng, body):
            for u in range(SLOTS):
                body(0, u, False)
            with eng.Fori(1, ITERS - 1) as it:
                for u in range(SLOTS):
                    body(it, u, False)
            for u in range(SLOTS):
                body(ITERS - 1, u, True)

        def buckets_from(engine, key, g0, n):
            return list(nc.values_load_multi_w_load_instructions(
                bucket_of[key][0:1, bass.ds(g0, n)], engines=[engine], min_val=0, max_val=BUCKETS - 1,
                skip_runtime_bounds_check_because="bucket_of holds bucket numbers, at most BUCKETS - 1")[1])

        def ahead(it, u, n, last):
            first = isinstance(it, int) and it == 0
            if (first and u + n < 0) or (last and u + n >= SLOTS):
                return None
            return it + (u + n) // SLOTS, (u + n) % SLOTS

        block = ctx.enter_context(nc.Block())

        @block.sync
        def _(sp):
            for tile, name in weights:
                sp.dma_start(tile[:, :], a[name]).then_inc(weights_in, 16)
            sp.wait_ge(consts_dve, 1)
            sp.dma_start(x_n[:, 0:BUCKETS - 1, :],
                         a["x"][0:(BUCKETS - 1) * P, :].rearrange("(b p) f -> p b f", p=P)).then_inc(x_in, 16)
            sp.dma_start(x_n[0:LAST, BUCKETS - 1, :], a["x"][(BUCKETS - 1) * P:N_NODES, :]).then_inc(x_in, 16)
            for n, k in enumerate(("dst", "src")):
                if n:
                    sp.wait_ge(hi_ready, n)
                sp.dma_start(idx_all, a[k].rearrange("(p j) -> p j", p=P)).then_inc(idx_in, 16)
                sp.wait_ge(hi_ready, n + 1)
                sp.dma_start(bucket_rows[k].rearrange("(p j) -> p j", p=P),
                             hi_bf[n][:, 0:N_EDGES // P]).then_inc(hi_out, 16)
            sp.wait_ge(pad_ready, 1)
            for k in ("dst", "src"):
                rows = recs[k].rearrange("(n p r) f -> n p (r f)", p=P, r=PAD_ROWS)
                for n in range(PAD_DMAS):
                    sp.dma_start(rows[n], pad_rec[k]).then_inc(pads_out, 16)
            sp.wait_ge(hi_out, 32)

            def hi_row(k, c):
                return bucket_rows[k][bass.ds(c * CHUNK, CHUNK)].partition_broadcast(BUCKETS)

            for k in ("dst", "src"):
                def load(c2, s):
                    sp.wait_ge(counted[s], chunk_turns(k, c2, s))
                    sp.nop(nofuse=True)
                    sp.dma_start(hi_in[s][0:BUCKETS, :], hi_row(k, c2 * 2 + s)).then_inc(count_in[s], 16)
                chunk_loop(sp, load)
            sp.wait_ge(tables_read, 1)
            for k in ("dst", "src"):
                other, attr, width, last = ("src", "edge_attr_13", 13, "edge_type_8") if k == "dst" else \
                    ("dst", "edge_attr_8", EDGE_D, "edge_weight")

                def load(c2, s):
                    c = c2 * 2 + s
                    sp.wait_ge(hi_used[s], chunk_turns(k, c2, s))
                    sp.nop(nofuse=True)
                    sp.dma_start(hi_in[s][0:BUCKETS, :], hi_row(k, c)).then_inc(keys_in[s], 16)
                    sp.wait_ge(where_ready[s], chunk_turns(k, c2, s))
                    sp.nop(nofuse=True)
                    for tile, name in ((key_in, k), (other_in, other), (last_in, last)):
                        src_ap = a[name][bass.ds(c * CHUNK, CHUNK)].rearrange("(p j) -> p j", p=P)
                        if name == "edge_weight":
                            src_ap = src_ap.bitcast(I32)
                        sp.dma_start(tile[:, s, :], src_ap).then_inc(keys_in[s], 16)
                    if k == "src":
                        sp.wait_ge(attr_copied[s], c2 + 1)
                        sp.nop(nofuse=True)
                    sp.dma_start(attr_in[:, s, 0:J * width],
                                 a[attr][bass.ds(c * CHUNK, CHUNK), :].rearrange("(p j) f -> p (j f)", p=P)
                                 ).then_inc(keys_in[s], 16)
                chunk_loop(sp, load)
            for s in range(2):
                sp.wait_ge(records_out[s], 16 * J * chunk_turns("src", (CHUNKS - 1 - s) // 2, s))

            for p in ALL:
                sp.wait_ge(table_ready, p + 1)
                if p in (L0A, L0B, L2A, L3):
                    tab, t_in = tables[p], h_n
                elif p == L1:
                    tab, t_in = tables[p], wide
                else:
                    tab, t_in = tables[p].rearrange("(n r) f -> n (r f)", r=RELS), wide
                sp.dma_start(tab.rearrange("(b p) f -> p b f", p=P), t_in[:, :, :]).then_inc(table_out, 16)
                key = "dst" if p in BY_DST else "src"
                rows = recs[key].rearrange("(n p t) f -> n p (t f)", p=P, t=T)

                def load(it, u, last):
                    if p in (L0A, L0B) and not (isinstance(it, int) and it == 0):
                        sp.wait_ge(*rest_ready.done(p, it, u, 2))
                    else:
                        sp.wait_ge(*read.done(p, it, u, SLOTS))
                    sp.nop(nofuse=True)
                    sp.dma_start(rec[key][:, u, :, :].rearrange("p t f -> p (t f)"),
                                 rows[bass.ds(it * SLOTS + u, 1)].rearrange("n p w -> p (n w)")
                                 ).then_inc(rec_in.of(u), 16)
                block_loop(sp, load)
            sp.wait_ge(out_ready, 1)
            sp.dma_start(out[0:(BUCKETS - 1) * P, :].rearrange("(b p) f -> p b f", p=P),
                         x_n[:, 0:BUCKETS - 1, :]).then_inc(out_done, 16)
            sp.dma_start(out[(BUCKETS - 1) * P:N_NODES, :], x_n[0:LAST, BUCKETS - 1, :]).then_inc(out_done, 16)
            sp.wait_ge(out_done, 32)

        @block.gpsimd
        def _(pool):
            pool.iota(iota_p[:, :], pattern=[[0, 1]], base=0, channel_multiplier=1,
                      allow_small_or_imprecise_dtypes=True)
            pool.iota(iota_f[:, :], pattern=[[1, P]], base=0, channel_multiplier=0,
                      allow_small_or_imprecise_dtypes=True)
            pool.iota(iota_g[:, :], pattern=[[1, GROUPS]], base=0, channel_multiplier=0,
                      allow_small_or_imprecise_dtypes=True)
            pool.drain().then_inc(consts_pool, 1)

            pool.wait_ge(pads_out, 16 * 2 * PAD_DMAS)
            for k in ("dst", "src"):
                def scatter(c2, s):
                    if k == "src":
                        pool.wait_ge(attr_copied[s], c2 + 2)
                        pool.nop(nofuse=True)
                    pool.wait_ge(where_ready[s], chunk_turns(k, c2, s) + 1)
                    pool.nop(nofuse=True)
                    for j in range(J):
                        pool.indirect_dma_start(
                            recs[k], bass.IndirectOffsetOnAxis(ap=where[:, s, j:j + 1], axis=0),
                            rec_out[:, s, j, 0:REC[k]], None).then_inc(records_out[s], 16)
                chunk_loop(pool, scatter)

            for p in ALL:
                pool.wait_ge(table_out, 16 * (p + 1))
                width = TABLE_W[p]
                key = "dst" if p in BY_DST else "src"
                column = (C_LAST if p == L2B else C_OTHER)[key]

                def gather(it, u, last):
                    pool.wait_ge(*rec_in.done(p, it, u))
                    pool.nop(nofuse=True)
                    for t in range(T):
                        pool.indirect_dma_start(
                            got[:, u, t, 0:width], None, tables[p],
                            bass.IndirectOffsetOnAxis(ap=rec[key][:, u, t, column:column + 1].bitcast(I32), axis=0),
                        ).then_inc(gathered[p].of(u), 16)
                block_loop(pool, gather)

        @block.scalar
        def _(act):
            for s in range(2):
                act.sem_inc(attr_copied[s], 1)

            def copy(c2, s):
                act.wait_ge(keys_in[s], 80 * chunk_turns("src", c2, s))
                act.wait_ge(records_out[s], 16 * J * (chunk_turns("src", c2, s) - 1))
                act.activation(rec_out[:, s, :, 0:EDGE_D],
                               attr_in[:, s, 0:J * EDGE_D].rearrange("p (j f) -> p j f", j=J),
                               ACT.Copy).then_inc(attr_copied[s], 1)
            chunk_loop(act, copy)

            def node(n, k_rows):
                act.wait_ge(node_src, n + 1)
                src = {N_GRU0: node_in, N_GRU1: node_in, N_Y: node_in, N_UPD: node_in, N_UPD2: node_in,
                       N_ROOT1: node_in, N_REL1: wide, N_Z: node_in, N_ROOT2: node_in}[n]
                with act.Fori(0, NODE_STEPS) as i:
                    act.wait_ge(node_used, i + (n * NODE_STEPS + 1))
                    act.activation(stage[:, :, 0:k_rows], src[:, bass.ds(i * NODE_TILES, NODE_TILES), 0:k_rows],
                                   ACT.Copy).then_inc(staged, 1)
                    act.wait_ge(node_turned, i + (n * NODE_STEPS + 1))
                    act.activation(turned[0:k_rows, :], ps_turn[0:k_rows, 0:NODE_TILES * P],
                                   ACT.Copy).then_inc(turned_ready, 1)
                    if n == N_UPD:
                        act.wait_ge(lin_done, i + 1)
                        act.activation(lin_t[:, :], ps_out[0:D, 0:NODE_TILES * P], ACT.Copy,
                                       scale=NORM_LIN).then_inc(lin_ready, 1)

            n_to = [0]

            def unary(dst, src, func, scale=1.0, bias=0.0):
                n_to[0] += 1
                act.wait_ge(to_act, n_to[0])
                act.activation(dst, src, func, scale=scale, bias=bias).then_inc(from_act, 1)

            def root():
                unary(stat[:, 2, :], stat[:, 1, :], ACT.Sqrt)

            def l0_pass(p):
                act.wait_ge(pass_open, p + 1)

                def step(it, u, last):
                    if at := ahead(it, u, 1, last):
                        act.wait_ge(*hid_turned.done(p, *at))
                        act.activation(hid_t[:, at[1] % 2, :], ps_turn_bf[0:HID_W, :],
                                       ACT.Copy).then_inc(hid_ready.of(at[1]), 1)
                    if at := ahead(it, u, 3, last):
                        act.wait_ge(*attr_turned.done(p, *at))
                        act.activation(attr_t[:, at[1] % 2, :], ps_turn_bf[0:ATTR_W, :],
                                       ACT.Copy).then_inc(attr_ready.of(at[1]), 1)
                    if at := ahead(it, u, 2, last):
                        v = at[1] % 2
                        act.wait_ge(*rest_ready.done(p, *at))
                        act.activation(hid_parts[:, v, :, HID:2 * HID], hid_rest[:, v, :, :],
                                       ACT.Copy).then_inc(mid_ready.of(at[1]), 1)
                    if at := ahead(it, u, 3, last):
                        v = at[1] % 2
                        act.wait_ge(*hid_done.done(p, *at))
                        act.activation(hid[:, v, :, :], ps_hid, ACT.Relu)
                        act.activation(hid_parts[:, v, :, 0:HID], ps_hid, ACT.Relu).then_inc(relu_ready.of(at[1]), 1)
                for u in range(-3, 0):
                    step(0, u, False)
                block_loop(act, step)

            act.wait_ge(weights_in, 16 * len(weights))
            root()
            for p, n in ((L0A, N_GRU0), (L0B, N_GRU1)):
                l0_pass(p)
                node(n, 2 * D + 2)
                unary(gates[:, :, 0:2 * D], gates[:, :, 0:2 * D], ACT.Sigmoid)
                unary(t_n[:, :, :], t_n[:, :, :], ACT.Tanh)
            root()
            node(N_Y, D)
            act.wait_ge(pass_open, L1 + 1)

            def silu(it, u, last):
                act.wait_ge(*read.done(L1, it, u))
                act.wait_ge(*scattered.done(L1, it, u, 2))
                act.activation(msg16[:, u % 2, :, :], small[:, u % 2, :, :], ACT.Silu,
                               scale=NORM_MSG).then_inc(silu_ready.of(u), 1)
            for u in range(SLOTS):
                act.sem_inc(silu_ready.of(u), 1)
            block_loop(act, silu)
            node(N_UPD, D)
            unary(node_in[:, :, 0:D], t_n[:, :, :], ACT.Silu, scale=NORM_UPD)
            node(N_UPD2, D)
            root()
            node(N_ROOT1, D + 1)
            node(N_REL1, P)
            node(N_Z, HID)
            node(N_ROOT2, HID + 1)
            root()
            act.wait_ge(pass_open, L3 + 1)

            def turn_onehot(it, u):
                act.wait_ge(*oh_turned.done(L3, it, u))
                act.activation(onehot_t[:, u % 2, :], ps_oht[:, :], ACT.Copy).then_inc(oht_ready.of(u), 1)
            turn_onehot(0, 0)

            def step(it, u, last):
                if at := ahead(it, u, 1, last):
                    turn_onehot(*at)
            block_loop(act, step)

        @block.vector
        def _(dve):
            dve.memset(x_n[:, BUCKETS - 1, :], 0.0)
            dve.memset(hid_parts[:, :, :, PARTS * HID:HID_W], 1.0)
            dve.memset(ones[:, :], 1.0)
            for k in ("dst", "src"):
                dve.memset(pad_rec[k], 0.0)
            dve.memset(rec_out[:, :, :, :], 0.0)
            dve.memset(msg_parts[:, :, :, :, D:D + 1], 0.0)
            dve.memset(agg17[:, :, :], 0.0)
            dve.drain()
            for k in ("dst", "src"):
                lane = C_LANE[k]
                dve.memset(pad_rec[k].rearrange("p (r f) -> p r f", f=REC[k])[:, :, lane:lane + 1], PAD_LANE)
            dve.memset(msg_parts[:, :, 0, :, D:D + 1], 1.0)
            dve.memset(rec_out[:, :, :, 0:ATTR_W // 2].bitcast(BF16)[:, :, :, ATTR_W - 1:ATTR_W], 1.0)
            dve.wait_ge(consts_pool, 1)
            dve.tensor_scalar(ident[:, :], iota_f[:, :], iota_p[:, 0:1], None, ALU.is_equal)
            dve.tensor_copy(iota_bf[:, :], iota_f[:, :])
            dve.tensor_scalar(ident_bf[:, :], iota_f[:, :], iota_p[:, 0:1], None, ALU.is_equal)
            dve.tensor_scalar(upto[:, :], iota_f[:, :], iota_p[:, 0:1], None, ALU.is_ge)
            dve.drain().then_inc(consts_dve, 1)
            dve.drain().then_inc(pad_ready, 1)
            for n, k in enumerate(("dst", "src")):
                dve.wait_ge(idx_in, 16 * (n + 1))
                dve.tensor_scalar(hi_int, idx_all, 7, None, ALU.logical_shift_right)
                dve.drain()
                dve.tensor_copy(hi_bf[n][:, 0:N_EDGES // P], hi_int)
                dve.drain().then_inc(hi_ready, 1)

            for s in range(2):
                dve.sem_inc(counted[s], 1)
            for n, k in enumerate(("dst", "src")):
                def count(c2, s):
                    dve.wait_ge(count_in[s], 16 * chunk_turns(k, c2, s))
                    dve.tensor_scalar(eq[0:BUCKETS, :], hi_in[s][0:BUCKETS, :], iota_p[0:BUCKETS, 0:1], None,
                                      ALU.is_equal, ALU.add,
                                      accum_out=counts[0:BUCKETS, bass.ds(c2 * 2 + s, 1)])
                    dve.drain().then_inc(counted[s], 1)
                chunk_loop(dve, count)
                ng = n_groups[k][0:BUCKETS, :]
                dve.tensor_reduce(ng, counts[0:BUCKETS, :], AX.X, ALU.add)
                dve.drain()
                dve.tensor_scalar(n_i[0:BUCKETS, :], ng, float(GROUP - 1), None, ALU.add)
                dve.drain()
                dve.tensor_scalar(n_i[0:BUCKETS, :], n_i[0:BUCKETS, :], GROUP.bit_length() - 1, None,
                                  ALU.logical_shift_right)
                dve.drain()
                dve.tensor_copy(ng, n_i[0:BUCKETS, :])
                dve.drain().then_inc(n_groups_ready, 1)
                dve.wait_ge(ends_ready, n + 1)
                dve.tensor_copy(end_g[0:BUCKETS, :], ps_end[0:BUCKETS, :])
                dve.drain()
                dve.tensor_scalar(carry[k][0:BUCKETS, :], end_g[0:BUCKETS, :], ng, float(GROUP),
                                  ALU.subtract, ALU.mult)
                dve.tensor_scalar(started[0:BUCKETS, :], iota_g[0:BUCKETS, :], end_g[0:BUCKETS, 0:1], None,
                                  ALU.is_ge)
                dve.drain().then_inc(started_ready, 1)
                dve.wait_ge(bucket_ready, 2 * n + 1)
                dve.tensor_scalar(bucket_of[k][:, :], ps_bucket[0:1, 0:GROUPS], float(BUCKETS - 1), None, ALU.min)
                dve.drain().then_inc(bucket_ready, 1)
            dve.drain().then_inc(tables_read, 1)

            for s in range(2):
                dve.sem_inc(hi_used[s], 1)
                dve.sem_inc(where_ready[s], 1)
            for k in ("dst", "src"):
                def place(c2, s):
                    dve.wait_ge(keys_in[s], 80 * chunk_turns(k, c2, s))
                    dve.tensor_scalar(eq[0:BUCKETS, :], hi_in[s][0:BUCKETS, :], iota_p[0:BUCKETS, 0:1], None,
                                      ALU.is_equal)
                    dve.drain().then_inc(hi_used[s], 1)
                    dve.tensor_tensor_scan(cum[0:BUCKETS, :], eq[0:BUCKETS, :], eq[0:BUCKETS, :],
                                           carry[k][0:BUCKETS, 0:1], ALU.add, ALU.max)
                    dve.drain()
                    dve.tensor_copy(carry[k][0:BUCKETS, :], cum[0:BUCKETS, CHUNK - 1:CHUNK])
                    dve.scalar_tensor_tensor(picked[s][0:BUCKETS, :], cum[0:BUCKETS, :], -1.0, eq[0:BUCKETS, :],
                                             ALU.add, ALU.mult)
                    dve.tensor_scalar(lane_i[:, :], key_in[:, s, :], P - 1, None, ALU.bitwise_and)
                    dve.drain().then_inc(picked_ready[s], 1)
                    if not (k == "dst" and isinstance(c2, int) and c2 == 0):
                        dve.wait_ge(records_out[s], 16 * J * (chunk_turns(k, c2, s) - 1))
                    out_i = rec_out[:, s, :, :].bitcast(I32)
                    dve.tensor_copy(rec_out[:, s, :, C_LANE[k]], lane_i[:, :])
                    dve.tensor_copy(out_i[:, :, C_OTHER[k]], other_in[:, s, :])
                    if k == "dst":
                        dve.tensor_scalar(pos_b[:, :], other_in[:, s, :], 3, None, ALU.logical_shift_left)
                        attr = attr_in[:, s, :].rearrange("p (j f) -> p j f", j=J)
                        parts = rec_out[:, s, :, 0:ATTR_W // 2].bitcast(BF16)
                        dve.tensor_copy(parts[:, :, 0:ATTR_D], attr)
                        dve.drain()
                        dve.tensor_tensor(out_i[:, :, C_LAST[k]], pos_b[:, :], last_in[:, s, :], ALU.bitwise_or)
                        dve.tensor_tensor(attr_rest[:, :, :], attr, parts[:, :, 0:ATTR_D], ALU.subtract)
                        dve.drain()
                        dve.tensor_copy(parts[:, :, ATTR_D:2 * ATTR_D], attr_rest[:, :, :])
                        dve.drain()
                        dve.tensor_tensor(parts[:, :, 2 * ATTR_D:3 * ATTR_D], attr_rest[:, :, :],
                                          parts[:, :, ATTR_D:2 * ATTR_D], ALU.subtract)
                    else:
                        dve.tensor_copy(out_i[:, :, C_LAST[k]], last_in[:, s, :])
                    dve.wait_ge(pos_ready[s], chunk_turns(k, c2, s))
                    dve.tensor_copy(pos_i[:, :], ps_pos[s][:, :])
                    dve.drain()
                    dve.tensor_scalar(pos_b[:, :], pos_i[:, :], GROUP - TILES_GROUP, 1, ALU.bitwise_and,
                                      ALU.logical_shift_left)
                    dve.tensor_scalar(pos_c[:, :], pos_i[:, :], GROUP, 7, ALU.bitwise_and,
                                      ALU.logical_shift_right)
                    dve.tensor_scalar(pos_i[:, :], pos_i[:, :], (1 << 24) - BLOCK + 1, None, ALU.bitwise_and)
                    dve.drain()
                    dve.tensor_tensor(pos_b[:, :], pos_b[:, :], pos_c[:, :], ALU.bitwise_or)
                    dve.drain()
                    dve.tensor_tensor(where[:, s, :], pos_b[:, :], pos_i[:, :], ALU.bitwise_or)
                    dve.drain().then_inc(where_ready[s], 1)
                chunk_loop(dve, place)

            n_act = [0]

            def through_act():
                n_act[0] += 1
                dve.drain().then_inc(to_act, 1)
                dve.wait_ge(from_act, n_act[0])

            def per_node(v):
                return v.unsqueeze(2).to_broadcast([P, BUCKETS, D])

            def layernorm_relu():
                dve.tensor_reduce(stat[:, 0, :], x_n[:, :, :], AX.X, ALU.add)
                dve.drain()
                dve.tensor_scalar(stat[:, 0, :], stat[:, 0, :], 1.0 / D, None, ALU.mult)
                dve.drain()
                dve.tensor_tensor(h_n[:, :, :], x_n[:, :, :], per_node(stat[:, 0, :]), ALU.subtract)
                dve.drain()
                dve.tensor_tensor(t_n[:, :, :], h_n[:, :, :], h_n[:, :, :], ALU.mult)
                dve.drain()
                dve.tensor_reduce(stat[:, 1, :], t_n[:, :, :], AX.X, ALU.add)
                dve.drain()
                dve.tensor_scalar(stat[:, 1, :], stat[:, 1, :], 1.0 / D, LN_EPS, ALU.mult, ALU.add)
                through_act()
                dve.reciprocal(stat[:, 2, :], stat[:, 2, :])
                dve.drain()
                dve.tensor_tensor(h_n[:, :, :], h_n[:, :, :], per_node(stat[:, 2, :]), ALU.mult)
                dve.drain()
                dve.tensor_scalar(h_n[:, :, :], h_n[:, :, :], 0.0, None, ALU.max)
                dve.drain()

            def node(n, consume):
                dve.drain().then_inc(node_src, 1)
                with dve.Fori(0, NODE_STEPS) as i:
                    dve.wait_ge(node_out, i + (n * NODE_STEPS + 1))
                    consume(bass.ds(i * NODE_TILES, NODE_TILES))
                    dve.drain().then_inc(node_used, 1)

            def product(width):
                return ps_out[:, 0:NODE_TILES * width].rearrange("p (t f) -> p t f", t=NODE_TILES)

            def make_onehot(key, u):
                v = u % 2
                dve.tensor_tensor(onehot[:, v, :, :], iota_f[:, :].unsqueeze(1).to_broadcast([P, T, P]),
                                  rec[key][:, u, :, C_LANE[key]:C_LANE[key] + 1].to_broadcast([P, T, P]), ALU.is_equal)

            def turn_buckets(p, it, first=0):
                key = "dst" if p in BY_DST else "src"
                return [None] * (first * GROUPS_BLOCK) + buckets_from(
                    mybir.EngineType.DVE, key, (it * SLOTS - 1 + first) * GROUPS_BLOCK, (SLOTS - first) * GROUPS_BLOCK)

            def add_group(it, u, back, g, bucket, sums, width):
                to = sums[:, bass.ds(bucket, 1), :].rearrange("p b f -> p (b f)")
                dve.tensor_tensor(to, to, acc((u - back) % 2, width)[:, g, :], ALU.add)

            def add_sums(p, it, u, buckets, sums, width):
                dve.wait_ge(*scattered.done(p, it, u, 1))
                for g in range(GROUPS_BLOCK):
                    add_group(it, u, 1, g, buckets[u * GROUPS_BLOCK + g], sums, width)
                    done = dve.drain()
                done.then_inc(added.of((u - 1) % SLOTS), 1)

            def edge_loop(p, step, sums, width, run_up=0):
                dve.drain().then_inc(pass_open, 1)
                for u in range(-run_up, 0):
                    step(0, u, False, lambda: None)

                def turn(it, last, first=0):
                    buckets = turn_buckets(p, it, first)
                    for u in range(SLOTS):
                        step(it, u, last, lambda: u < first or add_sums(p, it, u, buckets, sums, width))
                turn(0, False, 1)
                with dve.Fori(1, ITERS - 1) as it:
                    turn(it, False)
                turn(ITERS - 1, True)
                buckets = buckets_from(mybir.EngineType.DVE, "dst" if p in BY_DST else "src",
                                       GROUPS - GROUPS_BLOCK, GROUPS_BLOCK)
                add_sums(p, ITERS, 0, buckets, sums, width)

            for u in range(SLOTS):
                for s in (read, added):
                    dve.sem_inc(s.of(u), 1)
            dve.sem_inc(node_used, 1)

            dve.wait_ge(weights_in, 16 * len(weights))
            for w, parts in ((w1, w1_parts), (w2, w2_parts)):
                for n in range(PARTS):
                    dve.tensor_copy(parts[:, n, :], w[:, :])
                    dve.drain()
                    if n < PARTS - 1:
                        dve.tensor_tensor(w[:, :], w[:, :], parts[:, n, :], ALU.subtract)
                        dve.drain()
            dve.wait_ge(x_in, 32)
            layernorm_relu()
            dve.drain().then_inc(table_ready, 1)
            dve.memset(node_in[:, :, 2 * D:2 * D + 2], 1.0)
            for p, n in ((L0A, N_GRU0), (L0B, N_GRU1)):
                def step(it, u, last, buckets):
                    now, soon, late = ahead(it, u, 0, last), ahead(it, u, 2, last), ahead(it, u, -1, last)
                    then, done2 = ahead(it, u, 1, last), ahead(it, u, -2, False)
                    v, v1 = u % 2, (u - 1) % 2
                    if now:
                        dve.wait_ge(*gathered[p].done(p, *now))
                        dve.wait_ge(*w_done.done(p, *now))
                        dve.tensor_tensor(prod[:, :, :].rearrange("p t (i o) -> p t i o", i=D),
                                          ps_w[v].rearrange("p t (i o) -> p t i o", i=D),
                                          got[:, u, :, 0:D].unsqueeze(3).to_broadcast([P, T, D, D]), ALU.mult)
                    if late:
                        dve.tensor_copy(msg_parts[:, v1, 0, :, 0:D], msg[:, v1, :, :])
                    if soon:
                        vs = soon[1] % 2
                        dve.wait_ge(*relu_ready.done(p, *soon))
                        dve.tensor_tensor(hid_rest[:, vs, :, :], hid[:, vs, :, :], hid_parts[:, vs, :, 0:HID],
                                          ALU.subtract)
                    done = dve.drain()
                    if soon:
                        done.then_inc(rest_ready.of(soon[1]), 1)
                    if late:
                        dve.tensor_tensor(msg_rest[:, v1, :, :], msg[:, v1, :, :], msg_parts[:, v1, 0, :, 0:D],
                                          ALU.subtract)
                    if now:
                        dve.tensor_reduce(msg[:, v, :, :], prod[:, :, :].rearrange("p t (i o) -> p t o i", i=D),
                                          AX.X, ALU.add)
                    if then:
                        dve.wait_ge(*rec_in.done(p, *then))
                        for t in range(T):
                            lane = rec["dst"][:, then[1], t, C_LANE["dst"]:C_LANE["dst"] + 1]
                            dve.tensor_scalar(onehot_bf[:, then[1], t, :], iota_bf[:, :], lane, None, ALU.is_equal)
                    done = dve.drain()
                    if now:
                        done.then_inc(read.of(u), 1)
                    if late:
                        dve.tensor_copy(msg_parts[:, v1, 1, :, 0:D], msg_rest[:, v1, :, :])
                    if soon:
                        dve.wait_ge(*mid_ready.done(p, *soon))
                        dve.tensor_tensor(hid_parts[:, vs, :, 2 * HID:3 * HID], hid_rest[:, vs, :, :],
                                          hid_parts[:, vs, :, HID:2 * HID], ALU.subtract)
                    done = dve.drain()
                    if soon:
                        done.then_inc(parts_ready.of(soon[1]), 1)
                    if late:
                        dve.tensor_tensor(msg_parts[:, v1, 2, :, 0:D], msg_rest[:, v1, :, :],
                                          msg_parts[:, v1, 1, :, 0:D], ALU.subtract)
                    if done2:
                        dve.wait_ge(*scattered.done(p, *done2))
                        add_group(it, u, 2, 0, buckets[u * GROUPS_BLOCK], agg17, D + 1)
                    done = dve.drain()
                    if late:
                        done.then_inc(msg_split.of(late[1]), 1)
                    if done2:
                        for g in range(1, GROUPS_BLOCK):
                            add_group(it, u, 2, g, buckets[u * GROUPS_BLOCK + g], agg17, D + 1)
                            done = dve.drain()
                        done.then_inc(added.of(done2[1]), 1)

                def turn(it, first, last):
                    steps = SLOTS + 2 * last
                    lead = 2 * first
                    buckets = [None] * (lead * GROUPS_BLOCK) + buckets_from(
                        mybir.EngineType.DVE, "dst", (it * SLOTS - 2 + lead) * GROUPS_BLOCK,
                        (steps - lead) * GROUPS_BLOCK)
                    for u in range(steps):
                        step(it, u, last, buckets)

                dve.drain().then_inc(pass_open, 1)
                for u in range(-2, 0):
                    step(0, u, False, None)
                turn(0, True, False)
                with dve.Fori(1, ITERS - 1) as it:
                    turn(it, False, False)
                turn(ITERS - 1, False, True)
                dve.tensor_scalar(stat[:, 0, :], agg17[:, :, D], 1.0, None, ALU.max)
                dve.drain()
                dve.reciprocal(stat[:, 0, :], stat[:, 0, :])
                dve.drain()
                dve.tensor_tensor(node_in[:, :, 0:D], agg16, per_node(stat[:, 0, :]), ALU.mult)
                dve.tensor_copy(node_in[:, :, D:2 * D], h_n[:, :, :])
                node(n, lambda b: dve.tensor_copy(gates[:, b, :], product(4 * D)))
                through_act()
                dve.tensor_tensor(t_n[:, :, :], gates[:, :, 0:D], gates[:, :, 3 * D:4 * D], ALU.mult)
                dve.drain()
                dve.tensor_tensor(t_n[:, :, :], t_n[:, :, :], gates[:, :, 2 * D:3 * D], ALU.add)
                through_act()
                dve.tensor_tensor(h_n[:, :, :], h_n[:, :, :], t_n[:, :, :], ALU.subtract)
                dve.drain()
                dve.tensor_tensor(h_n[:, :, :], h_n[:, :, :], gates[:, :, D:2 * D], ALU.mult)
                dve.drain()
                dve.tensor_tensor(h_n[:, :, :], h_n[:, :, :], t_n[:, :, :], ALU.add)
                dve.memset(agg17[:, :, :], 0.0)
                dve.drain()
                if p == L0A:
                    dve.drain().then_inc(table_ready, 1)
            dve.tensor_tensor(x_n[:, :, :], x_n[:, :, :], h_n[:, :, :], ALU.add)
            dve.drain()

            layernorm_relu()
            dve.tensor_copy(node_in[:, :, 0:D], h_n[:, :, :])
            node(N_Y, lambda b: dve.tensor_copy(wide[:, b, :], product(P)))
            dve.drain().then_inc(table_ready, 1)

            def step(it, u, last, add):
                v = u % 2
                dve.wait_ge(*scattered.done(L1, it, u, 2))
                dve.wait_ge(*rec_in.done(L1, it, u))
                make_onehot("src", u)
                dve.wait_ge(*gathered[L1].done(L1, it, u))
                pv = prod[:, :, 0:D * EDGE_D].rearrange("p t (h j) -> p t h j", h=D)
                dve.tensor_tensor(pv, got[:, u, :, :].rearrange("p t (h j) -> p t h j", h=D),
                                  rec["src"][:, u, :, 0:EDGE_D].unsqueeze(2).to_broadcast([P, T, D, EDGE_D]), ALU.mult)
                dve.drain()
                dve.wait_ge(*silu_ready.done(L1, it, u, 2))
                dve.tensor_reduce(small[:, v, :, :], pv, AX.X, ALU.add)
                dve.drain().then_inc(read.of(u), 1)
                add()
            edge_loop(L1, step, agg16, D)
            dve.tensor_copy(node_in[:, :, 0:D], agg16)
            dve.drain()
            dve.memset(agg17[:, :, :], 0.0)

            def bilinear(b):
                v = ps_v[:, 0:NODE_TILES * D * D].rearrange("p (t k i) -> p t k i", t=NODE_TILES, k=D)
                big_flat = big[:, :, :].rearrange("p b f -> p (b f)")[:, 0:NODE_TILES * D * D]
                big_flat = big_flat.rearrange("p (t k i) -> p t k i", t=NODE_TILES, k=D)
                dve.tensor_tensor(big_flat, v, h_n[:, b, :].unsqueeze(2).to_broadcast([P, NODE_TILES, D, D]),
                                  ALU.mult)
                dve.drain()
                dve.tensor_reduce(t_n[:, b, :], big_flat, AX.X, ALU.add)
            node(N_UPD, bilinear)
            through_act()
            node(N_UPD2, lambda b: dve.tensor_scalar(t_n[:, b, :], product(D), NORM_LIN, None, ALU.mult))
            dve.tensor_tensor(t_n[:, :, :], t_n[:, :, :], h_n[:, :, :], ALU.add)
            dve.drain()
            dve.tensor_tensor(x_n[:, :, :], x_n[:, :, :], t_n[:, :, :], ALU.add)
            dve.drain()

            layernorm_relu()
            dve.drain().then_inc(table_ready, 1)
            dve.tensor_copy(node_in[:, :, 0:D], h_n[:, :, :])
            dve.memset(node_in[:, :, D:D + 1], 1.0)
            root_part = gates[:, :, 0:HID]
            node(N_ROOT1, lambda b: dve.tensor_copy(gates[:, b, 0:HID], product(HID)))
            dve.memset(big[:, :, :], 0.0)

            for p in (L2A, L2B):
                width = W2A if p == L2A else RELS * D

                def step(it, u, last, add):
                    v = u % 2
                    dve.wait_ge(*scattered.done(p, it, u, 2))
                    dve.wait_ge(*rec_in.done(p, it, u))
                    make_onehot("dst", u)
                    dve.tensor_scalar(rel_i[:, :], rec["dst"][:, u, :, C_LAST["dst"]].bitcast(I32), RELS - 1, None,
                                      ALU.bitwise_and)
                    dve.drain()
                    mask = msgw[:, v, :, RELS * D:W2A]
                    dve.tensor_tensor(mask, iota_f[:, 0:RELS].unsqueeze(1).to_broadcast([P, T, RELS]),
                                      rel_i[:, :].unsqueeze(2).to_broadcast([P, T, RELS]), ALU.is_equal)
                    dve.drain()
                    dve.wait_ge(*gathered[p].done(p, it, u))
                    dve.tensor_tensor(msgw[:, v, :, 0:RELS * D].rearrange("p t (r f) -> p t r f", r=RELS),
                                      mask.unsqueeze(3).to_broadcast([P, T, RELS, D]),
                                      got[:, u, :, 0:D].unsqueeze(2).to_broadcast([P, T, RELS, D]), ALU.mult)
                    dve.drain().then_inc(read.of(u), 1)
                    add()
                edge_loop(p, step, big[:, :, 0:width], width)
                if p == L2A:
                    dve.tensor_scalar(inv[:, :, :], big[:, :, RELS * D:W2A], 1.0, None, ALU.max)
                    dve.drain()
                    dve.reciprocal(inv[:, :, :], inv[:, :, :])
                    dve.drain()
                for r in range(RELS):
                    part = big[:, :, r * D:(r + 1) * D]
                    dve.tensor_tensor(part, part, inv[:, :, r:r + 1].to_broadcast([P, BUCKETS, D]), ALU.mult)
                if p == L2A:
                    node(N_REL1, lambda b: dve.tensor_tensor(gates[:, b, 0:HID], product(HID), gates[:, b, 0:HID],
                                                             ALU.add))
                    dve.tensor_scalar(node_in[:, :, 0:HID], root_part, 0.0, None, ALU.max)
                    dve.memset(node_in[:, :, HID:HID + 1], 1.0)
                    node(N_Z, lambda b: dve.tensor_copy(wide[:, b, :], product(P)))
                    dve.drain().then_inc(table_ready, 1)
                    node(N_ROOT2, lambda b: dve.tensor_copy(t_n[:, b, :], product(D)))
                    dve.wait_ge(table_out, 16 * (L2B + 1))
                    dve.memset(big[:, :, 0:RELS * D], 0.0)
            dve.drain()
            dve.tensor_reduce(u_n[:, :, :], big[:, :, 0:RELS * D].rearrange("p b (r f) -> p b f r", r=RELS),
                              AX.X, ALU.add)
            dve.drain()
            dve.tensor_tensor(t_n[:, :, :], t_n[:, :, :], u_n[:, :, :], ALU.add)
            dve.drain()
            dve.tensor_tensor(x_n[:, :, :], x_n[:, :, :], t_n[:, :, :], ALU.add)
            dve.drain()

            layernorm_relu()
            dve.drain().then_inc(table_ready, 1)
            def next_onehot(it, u):
                dve.wait_ge(*scattered.done(L3, it, u, 2))
                dve.wait_ge(*rec_in.done(L3, it, u))
                make_onehot("src", u)
                dve.drain().then_inc(oh_ready.of(u), 1)

            def uptake(it, u, last, add):
                if at := ahead(it, u, 1, last):
                    next_onehot(*at)
                if u < 0:
                    return
                v = u % 2
                xj = got[:, u, :, 0:D]
                den, num = small[:, 0, :, :], small[:, 1, :, :]
                dve.wait_ge(*gathered[L3].done(L3, it, u))
                dve.tensor_scalar(den, xj, 0.1, 5.0, ALU.mult, ALU.add)
                dve.tensor_tensor(num, xj, rec["src"][:, u, :, C_LAST["src"]:C_LAST["src"] + 1].to_broadcast([P, T, D]), ALU.mult)
                dve.drain()
                dve.wait_ge(*xi_done.done(L3, it, u))
                dve.scalar_tensor_tensor(den, ps_xi[v], 0.9, den, ALU.mult, ALU.add)
                dve.tensor_tensor(num, num, ps_xi[v], ALU.mult)
                dve.drain()
                dve.reciprocal(den, den)
                dve.drain()
                dve.tensor_tensor(msg16[:, v, :, :], num, den, ALU.mult)
                dve.drain().then_inc(read.of(u), 1)
                add()
            edge_loop(L3, uptake, agg16, D, run_up=1)
            dve.tensor_scalar(t_n[:, :, :], h_n[:, :, :], -1.0 / 5.0, 1.0, ALU.mult, ALU.add)
            dve.tensor_scalar(u_n[:, :, :], h_n[:, :, :], 1.0, None, ALU.subtract)
            dve.drain()
            dve.tensor_tensor(t_n[:, :, :], t_n[:, :, :], h_n[:, :, :], ALU.mult)
            dve.drain()
            dve.tensor_tensor(t_n[:, :, :], t_n[:, :, :], u_n[:, :, :], ALU.mult)
            dve.drain()
            dve.scalar_tensor_tensor(t_n[:, :, :], t_n[:, :, :], 0.1, agg16, ALU.add, ALU.add)
            dve.drain()
            dve.tensor_tensor(x_n[:, :, :], x_n[:, :, :], t_n[:, :, :], ALU.add)
            dve.drain().then_inc(out_ready, 1)

        @block.tensor
        def _(pe):
            pe.wait_ge(consts_dve, 1)
            for n in range(2):
                pe.wait_ge(n_groups_ready, n + 1)
                pe.matmul(ps_end[0:BUCKETS, :], upto[0:BUCKETS, 0:BUCKETS],
                          n_groups["src" if n else "dst"][0:BUCKETS, :], start=True, stop=True).then_inc(ends_ready, 1)
                pe.wait_ge(started_ready, n + 1)
                for c in range(0, GROUPS, BANK):
                    e = min(c + BANK, GROUPS)
                    last = pe.matmul(ps_bucket[0:1, c:e], ones[0:BUCKETS, 0:1], started[0:BUCKETS, c:e],
                                     start=True, stop=True)
                last.then_inc(bucket_ready, 1)
            for k in ("dst", "src"):
                def collect(c2, s):
                    pe.wait_ge(picked_ready[s], chunk_turns(k, c2, s))
                    pe.wait_ge(where_ready[s], chunk_turns(k, c2, s))
                    cells = picked[s][0:BUCKETS, :].rearrange("b (p j) -> b j p", j=J)
                    for j in range(J):
                        last = pe.matmul(ps_pos[s][:, j:j + 1], cells[:, j, :], ones[0:BUCKETS, 0:1],
                                         start=True, stop=True)
                    last.then_inc(pos_ready[s], 1)
                chunk_loop(pe, collect)

            def scatter(p, it, u, rhs, width, ready):
                v = u % 2
                pe.wait_ge(*ready.done(p, it, u))
                pe.wait_ge(*added.done(p, it, u, 2))
                for g in range(GROUPS_BLOCK):
                    for t in range(TILES_GROUP):
                        tt = g * TILES_GROUP + t
                        last = pe.matmul(acc(v, width)[:, g, :], onehot[:, v, tt, :], rhs[:, v, tt, 0:width],
                                         start=(t == 0), stop=(t == TILES_GROUP - 1))
                last.then_inc(scattered.of(u), 1)

            def node(n, k_rows, w, width):
                with pe.Fori(0, NODE_STEPS) as i:
                    pe.wait_ge(staged, i + (n * NODE_STEPS + 1))
                    pe.nop(nofuse=True)
                    for t in range(NODE_TILES):
                        last = pe.transpose(ps_turn[0:k_rows, t * P:(t + 1) * P], stage[:, t, 0:k_rows], ident[:, :])
                    last.then_inc(node_turned, 1)
                    pe.wait_ge(turned_ready, i + (n * NODE_STEPS + 1))
                    pe.nop(nofuse=True)
                    if n == N_UPD:
                        for c in range(0, NODE_TILES * P, BANK):
                            e = min(c + BANK, NODE_TILES * P)
                            last = pe.matmul(ps_out[0:D, c:e], wlin[:, :], turned[0:D, c:e], start=True, stop=True)
                        last.then_inc(lin_done, 1)
                        pe.wait_ge(lin_ready, i + 1)
                        pe.nop(nofuse=True)
                    for t in range(NODE_TILES):
                        if n == N_UPD:
                            to, lhs = ps_v[:, t * D * D:(t + 1) * D * D], lin_t[:, t * P:(t + 1) * P]
                        else:
                            to, lhs = ps_out[:, t * width:(t + 1) * width], turned[0:k_rows, t * P:(t + 1) * P]
                        last = pe.matmul(to, lhs, w[:, :], start=True, stop=True)
                    last.then_inc(node_out, 1)

            for u in range(SLOTS):
                pe.sem_inc(scattered.of(u), 1)
            pe.wait_ge(weights_in, 16 * len(weights))

            for p, n in ((L0A, N_GRU0), (L0B, N_GRU1)):
                def step(it, u, last):
                    soon, later = ahead(it, u, 1, last), ahead(it, u, 3, last)
                    if soon:
                        vs = soon[1] % 2
                        pe.wait_ge(*parts_ready.done(p, *soon))
                        pe.nop(nofuse=True)
                        for t in range(T):
                            end = pe.transpose(ps_turn_bf[0:HID_W, t * P:(t + 1) * P],
                                               hid_parts[:, vs, t, 0:HID_W], ident_bf[:, :])
                        end.then_inc(hid_turned.of(soon[1]), 1)
                    if at := ahead(it, u, -2, False):
                        v = at[1] % 2
                        pe.wait_ge(*msg_split.done(p, *at))
                        pe.wait_ge(*added.done(p, *at, 2))
                        pe.nop(nofuse=True)
                        for g in range(GROUPS_BLOCK):
                            for t in range(g * TILES_GROUP, (g + 1) * TILES_GROUP):
                                for n in range(PARTS):
                                    end = pe.matmul(acc(v, D + 1)[:, g, :], onehot_bf[:, at[1], t, :],
                                                    msg_parts[:, v, n, t, :],
                                                    start=(t == g * TILES_GROUP and n == 0),
                                                    stop=(t == (g + 1) * TILES_GROUP - 1 and n == PARTS - 1))
                        end.then_inc(scattered.of(at[1]), 1)
                    if soon:
                        pe.wait_ge(*hid_ready.done(p, *soon))
                        pe.nop(nofuse=True)
                    if later:
                        pe.wait_ge(*rec_in.done(p, *later))
                        pe.nop(nofuse=True)
                        for t in range(T):
                            attr = rec["dst"][:, later[1], t, 0:ATTR_W // 2].bitcast(BF16)
                            end = pe.transpose(ps_turn_bf[0:ATTR_W, t * P:(t + 1) * P], attr, ident_bf[:, :])
                        end.then_inc(attr_turned.of(later[1]), 1)
                    if soon:
                        pe.wait_ge(*read.done(p, *soon, 2))
                        pe.nop(nofuse=True)
                        for t in range(T):
                            for n in range(PARTS):
                                end = pe.matmul(ps_w[vs][:, t, :], hid_t[:, vs, t * P:(t + 1) * P],
                                                w2_parts[:, n, :], start=(n == 0), stop=(n == PARTS - 1))
                        end.then_inc(w_done.of(soon[1]), 1)
                    if later:
                        pe.wait_ge(*attr_ready.done(p, *later))
                        pe.nop(nofuse=True)
                        for t in range(T):
                            for n in range(PARTS):
                                end = pe.matmul(ps_hid[:, t, :], attr_t[:, later[1] % 2, t * P:(t + 1) * P],
                                                w1_parts[:, n, :], start=(n == 0), stop=(n == PARTS - 1))
                        end.then_inc(hid_done.of(later[1]), 1)
                pe.wait_ge(pass_open, p + 1)
                for u in range(-3, 0):
                    step(0, u, False)
                for u in range(SLOTS):
                    step(0, u, False)
                with pe.Fori(1, ITERS - 1) as it:
                    for u in range(SLOTS):
                        step(it, u, False)
                for u in range(SLOTS + 2):
                    step(ITERS - 1, u, True)
                node(n, 2 * D + 2, wg, 4 * D)
            node(N_Y, D, wy, P)
            pe.wait_ge(pass_open, L1 + 1)
            block_loop(pe, lambda it, u, last: scatter(L1, it, u, msg16, D, silu_ready))
            node(N_UPD, D, wupd, D * D)
            node(N_UPD2, D, wupd2, D)
            node(N_ROOT1, D + 1, wroot1, HID)
            pe.wait_ge(pass_open, L2A + 1)
            block_loop(pe, lambda it, u, last: scatter(L2A, it, u, msgw, W2A, read))
            node(N_REL1, P, wrel1, HID)
            node(N_Z, HID, wz, P)
            node(N_ROOT2, HID + 1, wroot2, D)
            pe.wait_ge(pass_open, L2B + 1)
            block_loop(pe, lambda it, u, last: scatter(L2B, it, u, msgw, RELS * D, read))
            pe.wait_ge(pass_open, L3 + 1)

            def turn_onehot(it, u):
                pe.wait_ge(*oh_ready.done(L3, it, u))
                for t in range(T):
                    last = pe.transpose(ps_oht[:, t * P:(t + 1) * P], onehot[:, u % 2, t, :], ident[:, :])
                last.then_inc(oh_turned.of(u), 1)

            def sources(it, u, buckets):
                v = u % 2
                pe.wait_ge(*oht_ready.done(L3, it, u))
                pe.wait_ge(*read.done(L3, it, u, 2))
                for g in range(GROUPS_BLOCK):
                    for t in range(TILES_GROUP):
                        tt = g * TILES_GROUP + t
                        end = pe.matmul(ps_xi[v][:, tt, :], onehot_t[:, v, tt * P:(tt + 1) * P],
                                        h_n[:, bass.ds(buckets[g], 1), :].rearrange("p b f -> p (b f)"),
                                        start=True, stop=True)
                end.then_inc(xi_done.of(u), 1)

            def sources_turn(it, last):
                n = (SLOTS - last) * GROUPS_BLOCK
                buckets = buckets_from(mybir.EngineType.PE, "src", (it * SLOTS + 1) * GROUPS_BLOCK, n)
                for u in range(SLOTS):
                    at = ahead(it, u, 1, last)
                    if at:
                        turn_onehot(*at)
                    scatter(L3, it, u, msg16, D, read)
                    if at:
                        sources(*at, buckets[u * GROUPS_BLOCK:(u + 1) * GROUPS_BLOCK])
            turn_onehot(0, 0)
            sources(0, 0, buckets_from(mybir.EngineType.PE, "src", 0, GROUPS_BLOCK))
            sources_turn(0, False)
            with pe.Fori(1, ITERS - 1) as it:
                sources_turn(it, False)
            sources_turn(ITERS - 1, True)


def kernel(**inputs):
    import numpy as _np
    import concourse.bacc as _bacc
    from concourse import mybir as _mybir
    from concourse.bass_utils import run_bass_kernel_spmd as _run

    i = {k: _np.ascontiguousarray(v) for k, v in inputs.items()}
    ih, hh = i["L0_gnn_gru_w_ih"], i["L0_gnn_gru_w_hh"]
    arrays = {k: i[k] for k in ("x", "src", "dst", "edge_attr_13", "edge_attr_8", "edge_type_8", "edge_weight")}
    arrays["w1"] = _np.concatenate([i["L0_gnn_fnet_w1"]] * PARTS + [i["L0_gnn_fnet_b1"][None, :]], 0)
    arrays["w2"] = _np.concatenate([i["L0_gnn_fnet_w2"]] * PARTS + [i["L0_gnn_fnet_b2"][None, :]], 0)
    wg = _np.zeros((2 * D + 2, 4 * D), _np.float32)
    wg[0:D, 0:3 * D] = ih.T
    wg[D:2 * D, 0:2 * D], wg[D:2 * D, 3 * D:] = hh.T[:, :2 * D], hh.T[:, 2 * D:]
    wg[2 * D, 0:3 * D] = i["L0_gnn_gru_b_ih"]
    wg[2 * D + 1, 0:2 * D], wg[2 * D + 1, 3 * D:] = i["L0_gnn_gru_b_hh"][:2 * D], i["L0_gnn_gru_b_hh"][2 * D:]
    arrays["wg"] = wg
    arrays["wy"] = _np.ascontiguousarray(i["L1_gnn_W_msg_tp"].transpose(0, 2, 1)).reshape(D, D * EDGE_D)
    arrays["wlin"] = i["L1_gnn_W_msg_lin"]
    arrays["wupd"] = _np.ascontiguousarray(i["L1_gnn_W_upd_tp"].transpose(1, 2, 0)).reshape(D, D * D)
    arrays["wupd2"] = i["L1_gnn_W_upd_lin"]
    arrays["wroot1"] = _np.concatenate([i["L2_gnn_root1"], i["L2_gnn_b1"][None, :]], 0)
    arrays["wrel1"] = i["L2_gnn_W1"].reshape(RELS * D, HID)
    arrays["wz"] = _np.ascontiguousarray(i["L2_gnn_W2"].transpose(1, 0, 2)).reshape(HID, RELS * D)
    arrays["wroot2"] = _np.concatenate([i["L2_gnn_root2"], i["L2_gnn_b2"][None, :]], 0)

    nc = _bacc.Bacc("TRN2", target_bir_lowering=False, num_devices=1)
    args = {k: nc.dram_tensor(f"in_{k}", v.shape, _mybir.dt.from_np(v.dtype), kind="ExternalInput").ap()
            for k, v in arrays.items()}
    out = nc.dram_tensor("out", (N_NODES, D), _mybir.dt.float32, kind="ExternalOutput").ap()
    gnn_kernel(nc, args, out)
    r = _run(nc, [{f"in_{k}": v for k, v in arrays.items()}], core_ids=[0])
    return r.results[0]["out"]
```

```python
import concourse.bass as bass
from concourse import mybir
from contextlib import ExitStack

F32 = mybir.dt.float32
I32 = mybir.dt.int32
BF16 = mybir.dt.bfloat16
ALU = mybir.AluOpType
ACT = mybir.ActivationFunctionType
AX = mybir.AxisListType

P = 128
N_NODES = 12500
N_EDGES = 400000
D = 16
BUCKETS = -(-N_NODES // P)
N_PAD = BUCKETS * P
LAST = N_NODES - (BUCKETS - 1) * P

TILES_GROUP = 2
GROUP = TILES_GROUP * P
GROUPS_BLOCK = 2
T = TILES_GROUP * GROUPS_BLOCK
BLOCK = T * P
SLOTS = 4
MAX_GROUPS = (N_EDGES + BUCKETS * (GROUP - 1)) // GROUP
ITERS = -(-MAX_GROUPS // (GROUPS_BLOCK * SLOTS))
ITERS += -ITERS % 4
BLOCKS = ITERS * SLOTS
GROUPS = BLOCKS * GROUPS_BLOCK
ATTR_D = 13
PARTS = 3
ATTR_W = PARTS * ATTR_D + 1
REC = {"dst": 24, "src": 16}
C_LANE, C_OTHER, C_LAST = ({"dst": 20 + n, "src": 8 + n} for n in range(3))
PAD_LANE = 255.0

J = 25
CHUNK = P * J
CHUNKS = N_EDGES // CHUNK

COUNTS_CHUNK = -(-BUCKETS // CHUNKS)

HID = 32
HID_W = PARTS * HID + 1
RELS = 8
EDGE_D = 8
W2A = RELS * D + RELS
NODE_TILES = 7
NODE_STEPS = BUCKETS // NODE_TILES
PAD_ROWS = 64
LN_EPS = 1e-5
NORM_MSG = float((D * EDGE_D) ** -0.5)
NORM_UPD = float((D * D) ** -0.5)
NORM_LIN = float(D ** -0.5)

PAD_DMAS = BLOCKS * BLOCK // (P * PAD_ROWS)

L0A, L0B, L1, L2A, L2B, L3 = range(6)
BY_DST = (L0A, L0B, L2A, L2B)
TABLE_W = {L0A: D, L0B: D, L1: D * EDGE_D, L2A: D, L2B: D, L3: D}
(N_GRU0, N_GRU1, N_Y, N_UPD, N_UPD2, N_ROOT1, N_REL1, N_Z, N_ROOT2) = range(9)


def gnn_kernel(nc, a, out):
    ctx = ExitStack()
    with ctx:
        def sb(name, shape, dt=F32):
            return ctx.enter_context(nc.sbuf_tensor(name, shape, dt))

        def sem(name):
            return ctx.enter_context(nc.semaphore(name))

        def dram(name, shape, dt=F32):
            return nc.dram_tensor(name, shape, dt, kind="Internal").ap()

        bucket_rows = {"dst": dram("bucket_dst", (N_EDGES,), BF16), "src": dram("bucket_src", (N_EDGES,), BF16)}
        recs = {k: dram(f"rec_{k}", (BLOCKS * BLOCK, REC[k])) for k in ("dst", "src")}
        tables = {p: dram(f"table{p}", (N_PAD, TABLE_W[p])) for p in (L0A, L0B, L1, L2A, L3)}
        tables[L2B] = dram("table_rel", (N_PAD * RELS, D))

        x_n = sb("x_n", [P, BUCKETS, D])
        h_n = sb("h_n", [P, BUCKETS, D])
        t_n = sb("t_n", [P, BUCKETS, D])
        u_n = sb("u_n", [P, BUCKETS, D])
        stat = sb("stat", [P, 3, BUCKETS])
        inv = sb("inv", [P, BUCKETS, RELS])
        agg17 = sb("agg17", [P, BUCKETS, D + 1])
        agg16 = agg17[:, :, 0:D]
        big = sb("big", [P, BUCKETS, W2A])
        wide = big[:, :, 0:P]
        SORT_WORDS = 2 * CHUNK // 2 + CHUNK // 2 + CHUNK + 2 * CHUNK
        NODE_WORDS = BUCKETS * (2 * HID) + BUCKETS * (2 * D + 2)
        shared = sb("shared", [P, max(SORT_WORDS, NODE_WORDS + 5 * NODE_TILES * P)])
        o = 0
        hi_in = []
        for s in range(2):
            hi_in.append(shared[:, o:o + CHUNK // 2].bitcast(BF16))
            o += CHUNK // 2
        eq = shared[:, o:o + CHUNK // 2].bitcast(BF16)
        o += CHUNK // 2
        cum = shared[:, o:o + CHUNK]
        o += CHUNK
        picked = [shared[:, o + s * CHUNK:o + (s + 1) * CHUNK] for s in range(2)]
        gates = shared[:, 0:BUCKETS * 2 * HID].rearrange("p (b f) -> p b f", b=BUCKETS)
        node_in = shared[:, BUCKETS * 2 * HID:NODE_WORDS].rearrange("p (b f) -> p b f", b=BUCKETS)

        big_flat = big[:, :, :].rearrange("p b f -> p (b f)")
        idx_all = big_flat[:, 0:N_EDGES // P].bitcast(I32)
        hi_int = big_flat[:, N_EDGES // P:2 * (N_EDGES // P)].bitcast(I32)
        hi_words = (N_EDGES // P + 1) // 2
        hi_bf = [room[:, 0:hi_words].bitcast(BF16)[:, 0:N_EDGES // P] for room in (shared, big_flat)]
        pad_rec = {k: big_flat[:, o:o + PAD_ROWS * REC[k]]
                   for k, o in (("dst", 8192), ("src", 8192 + PAD_ROWS * REC["dst"]))}

        REC_WORDS = 2 * J * REC["dst"]
        rec_room = sb("rec_room", [P, max(REC_WORDS, 2 * BLOCK)])
        rec_out = rec_room[:, 0:REC_WORDS].rearrange("p (s j f) -> p s j f", s=2, j=J)
        onehot_t = rec_room[:, 0:2 * BLOCK].rearrange("p (v e) -> p v e", v=2)
        where = sb("where", [P, 2, J], I32)
        carry = {k: sb(f"carry_{k}", [P, 1]) for k in ("dst", "src")}
        n_groups = {k: sb(f"n_groups_{k}", [P, 1]) for k in ("dst", "src")}
        n_i = sb("n_i", [P, 1], I32)
        end_g = sb("end_g", [P, 1])
        iota_p = sb("iota_p", [P, 1])
        iota_f = sb("iota_f", [P, P])
        upto = sb("upto", [P, P])
        ones = sb("ones", [P, P])
        ident = sb("ident", [P, P])
        ident_bf = sb("ident_bf", [P, P], BF16)
        started = picked[0][:, 0:GROUPS]
        bucket_of = {k: sb(f"bucket_of_{k}", [1, GROUPS], I32) for k in ("dst", "src")}
        o = max(2 * (N_EDGES // P), CHUNK + CHUNK // 2)
        iota_g = big_flat[:, o:o + GROUPS]
        src_eq = big_flat[:, CHUNK:CHUNK + hi_words].bitcast(BF16)[:, 0:N_EDGES // P]

        rec = {k: sb(f"rec_{k}_in", [P, SLOTS, T, REC[k]]) for k in ("dst", "src")}
        got = sb("got", [P, SLOTS, T, D * EDGE_D])
        onehot_room = sb("onehot_room", [P, 2 * T * (P + W2A)])
        onehot = onehot_room[:, 0:2 * T * P].rearrange("p (v t f) -> p v t f", v=2, t=T)
        onehot4 = onehot_room[:, 0:SLOTS * T * P].rearrange("p (u t f) -> p u t f", u=SLOTS, t=T)
        onehot4_bf = onehot_room[:, 0:SLOTS * T * P].bitcast(BF16).rearrange(
            "p (u t f h) -> p u t f h", u=SLOTS, t=T, h=2)[:, :, :, :, 1]
        msgw = onehot_room[:, 2 * T * P:2 * T * (P + W2A)].rearrange("p (v t f) -> p v t f", v=2, t=T)
        got_flat = got[:, :, :, :].rearrange("p u t f -> p (u t f)")
        attr_in = got_flat[:, 0:2 * J * ATTR_D].rearrange("p (s f) -> p s f", s=2)
        o = 2 * J * ATTR_D
        key_in, other_in, last_in = (got_flat[:, o + n * 2 * J:o + (n + 1) * 2 * J].bitcast(I32)
                                     .rearrange("p (s j) -> p s j", s=2) for n in range(3))
        o += 3 * 2 * J
        lane_i, pos_i, pos_b, pos_c = (got_flat[:, o + n * J:o + (n + 1) * J].bitcast(I32) for n in range(4))
        counts = got_flat[:, o + 4 * J:o + 4 * J + CHUNKS * COUNTS_CHUNK]
        prod = sb("prod", [P, T, D * D])
        prod_flat = prod[:, :, :].rearrange("p t f -> p (t f)")
        attr_rest = prod_flat[:, 0:J * ATTR_D].rearrange("p (j f) -> p j f", j=J)
        msg = sb("msg", [P, 2, T, D])
        msg_rest = sb("msg_rest", [P, 2, T, D])
        msg_parts = sb("msg_parts", [P, SLOTS, PARTS, T, D + 1], BF16)
        onehot_bf = sb("onehot_bf", [P, SLOTS, T, P], BF16)
        msg16 = sb("msg16", [P, 2, T, D])
        rel_i = sb("rel_i", [P, T], I32)
        attr_t = sb("attr_t", [ATTR_W, 2, BLOCK], BF16)
        hid = sb("hid", [P, 2, T, HID])
        hid_rest = sb("hid_rest", [P, 2, T, HID])
        hid_parts = sb("hid_parts", [P, 2, T, HID_W + 1], BF16)
        hid_t = sb("hid_t", [HID_W, 2, BLOCK], BF16)
        small = sb("small", [P, 2, T, D])

        tile_words = NODE_TILES * P
        node_room = [shared[:, NODE_WORDS + n * tile_words:NODE_WORDS + (n + 1) * tile_words] for n in range(5)]
        stage = [r.rearrange("p (t f) -> p t f", t=NODE_TILES) for r in node_room[0:2]]
        turned = node_room[2:4]
        lin_t = node_room[4][0:D, :]

        w1 = sb("w1", [ATTR_W, HID])
        w2 = sb("w2", [HID_W, D * D])
        w1_parts = sb("w1_parts", [ATTR_W, PARTS, HID], BF16)
        w2_parts = sb("w2_parts", [HID_W, PARTS, D * D], BF16)
        wg = sb("wg", [2 * D + 2, 4 * D])
        wy = sb("wy", [D, D * EDGE_D])
        wlin = sb("wlin", [D, D])
        wupd = sb("wupd", [D, D * D])
        wupd2 = sb("wupd2", [D, D])
        wroot1 = sb("wroot1", [D + 1, HID])
        wrel1 = sb("wrel1", [P, HID])
        wz = sb("wz", [HID, P])
        wroot2 = sb("wroot2", [HID + 1, D])
        weights = [(w1, "w1"), (w2, "w2"), (wg, "wg"), (wy, "wy"), (wlin, "wlin"), (wupd, "wupd"),
                   (wupd2, "wupd2"), (wroot1, "wroot1"), (wrel1, "wrel1"), (wz, "wz"), (wroot2, "wroot2")]

        BANK = 512
        ps = ctx.enter_context(nc.psum_tensor("ps", [P, 8 * BANK], F32))
        ps_pos = [ps[:, s * BANK:s * BANK + J] for s in range(2)]
        ps_total = ps[:, 3 * BANK:3 * BANK + 1]
        ps_end = ps[:, 2 * BANK:2 * BANK + 1]
        ps_bucket = ps[:, 4 * BANK:8 * BANK]
        ps_turn_bf = ps[:, 0:BLOCK // 2].bitcast(BF16)
        ps_hid = ps[:, BANK:BANK + T * HID].rearrange("p (t f) -> p t f", t=T)
        ps_attr_bf = ps[:, BANK + T * HID:BANK + T * HID + BLOCK // 2].bitcast(BF16)
        ps_w = [ps[:, (2 + 2 * v) * BANK:(4 + 2 * v) * BANK].rearrange("p (t f) -> p t f", t=T) for v in range(2)]
        ps_acc = [ps[:, (6 + v) * BANK:(7 + v) * BANK] for v in range(2)]
        ps_oht = ps[:, 0:BLOCK // 2].bitcast(BF16)
        ps_xi = [ps[:, (2 + v) * BANK:(2 + v) * BANK + T * D].rearrange("p (t f) -> p t f", t=T) for v in range(2)]
        ps_turn = ps[:, 0:2 * BANK]
        ps_out = [ps[:, (2 + 2 * v) * BANK:(4 + 2 * v) * BANK] for v in range(2)]
        ps_v = ps[:, 4 * BANK:8 * BANK]

        def acc(v, width):
            return ps_acc[v][:, 0:GROUPS_BLOCK * width].rearrange("p (g f) -> p g f", g=GROUPS_BLOCK)

        consts_pool = sem("consts_pool")
        consts_dve = sem("consts_dve")
        weights_in = sem("weights_in")
        x_in = sem("x_in")
        idx_in = sem("idx_in")
        hi_ready = sem("hi_ready")
        hi_out = sem("hi_out")
        pad_ready = sem("pad_ready")
        pads_out = {k: sem(f"pads_out_{k}") for k in ("dst", "src")}
        counts_ready = sem("counts_ready")
        totals_ready = sem("totals_ready")
        n_groups_ready = sem("n_groups_ready")
        ends_ready = sem("ends_ready")
        started_ready = sem("started_ready")
        bucket_ready = sem("bucket_ready")
        tables_read = sem("tables_read")
        keys_in = [sem(f"keys_in{s}") for s in range(2)]
        hi_used = [sem(f"hi_used{s}") for s in range(2)]
        picked_ready = [sem(f"picked_ready{s}") for s in range(2)]
        pos_ready = [sem(f"pos_ready{s}") for s in range(2)]
        where_ready = [sem(f"where_ready{s}") for s in range(2)]
        attr_copied = [sem(f"attr_copied{s}") for s in range(2)]
        records_out = [sem(f"records_out{s}") for s in range(2)]

        L0_STEPS = BLOCKS + 6
        step_mark = sem("step_mark")

        def marked(p, it, u, back=0):
            return step_mark, it * SLOTS + (u - back + 3 + p * L0_STEPS)

        class Slots:

            def __init__(self, name, passes, unit=1, credit=0):
                self.sems = [sem(f"{name}{u}") for u in range(SLOTS)]
                self.passes, self.unit, self.credit = list(passes), unit, credit

            def of(self, u):
                return self.sems[u]

            def done(self, p, it, u, back=0):
                turns = it + (u - back) // SLOTS + 1 + self.passes.index(p) * ITERS
                return self.sems[(u - back) % SLOTS], turns * self.unit + self.credit

        ALL = [L0A, L0B, L1, L2A, L2B, L3]
        rec_in = Slots("rec_in", ALL, 16)
        early, late = Slots("gathered", ALL[:4], 16 * T), Slots("gathered_late", ALL[4:], 16 * T)
        gathered = {p: early if p in early.passes else late for p in ALL}
        read = Slots("read", ALL, 1, 1)
        scattered = Slots("scattered", ALL, 1, 1)
        added = Slots("added", ALL[2:5], 1, 1)
        attr_turned = Slots("attr_turned", (L0A, L0B))
        attr_ready = Slots("attr_ready", (L0A, L0B))
        hid_done = Slots("hid_done", (L0A, L0B))
        relu_ready = Slots("relu_ready", (L0A, L0B))
        mid_ready = Slots("mid_ready", (L0A, L0B))
        parts_ready = Slots("parts_ready", (L0A, L0B))
        oh_made = Slots("oh_made", (L0A, L0B))
        hid_turned = Slots("hid_turned", (L0A, L0B))
        hid_ready = Slots("hid_ready", (L0A, L0B))
        w_done = Slots("w_done", (L0A, L0B))
        silu_ready = Slots("silu_ready", (L1,), 1, 1)
        oh_ready = Slots("oh_ready", (L3,))
        oh_turned = Slots("oh_turned", (L3,))
        oht_ready = Slots("oht_ready", (L3,))
        xi_done = Slots("xi_done", (L3,))

        pass_open = sem("pass_open")
        table_ready = sem("table_ready")
        table_out = sem("table_out")
        node_src = sem("node_src")
        staged = sem("staged")
        node_turned = sem("node_turned")
        turned_ready = sem("turned_ready")
        lin_done = sem("lin_done")
        lin_ready = sem("lin_ready")
        node_out = sem("node_out")
        node_used = sem("node_used")
        to_act = sem("to_act")
        from_act = sem("from_act")
        out_ready = sem("out_ready")
        out_done = sem("out_done")

        COUNT_TURNS = {"dst": 0, "src": 1}

        def chunk_turns(k, c2, s):
            return COUNT_TURNS[k] * ((CHUNKS + 1 - s) // 2) + c2 + 1

        def chunk_loop(eng, body):
            for s in range(2):
                body(0, s)
            with eng.Fori(1, CHUNKS // 2) as c2:
                for s in range(2):
                    body(c2, s)
            body(CHUNKS // 2, 0)

        def block_loop(eng, body):
            for u in range(SLOTS):
                body(0, u, False)
            with eng.Fori(1, ITERS - 1) as it:
                for u in range(SLOTS):
                    body(it, u, False)
            for u in range(SLOTS):
                body(ITERS - 1, u, True)

        def node_loop(eng, body):
            with eng.Fori(0, NODE_STEPS // 2 - 1) as pair:
                for v in range(2):
                    body(pair * 2 + v, v, False)
            for v in range(2):
                body(NODE_STEPS - 2 + v, v, v == 1)

        def buckets_from(engine, key, g0, n):
            return list(nc.values_load_multi_w_load_instructions(
                bucket_of[key][0:1, bass.ds(g0, n)], engines=[engine], min_val=0, max_val=BUCKETS - 1,
                skip_runtime_bounds_check_because="bucket_of holds bucket numbers, at most BUCKETS - 1")[1])

        def ahead(it, u, n, last):
            first = isinstance(it, int) and it == 0
            if (first and u + n < 0) or (last and u + n >= SLOTS):
                return None
            return it + (u + n) // SLOTS, (u + n) % SLOTS

        def sweep(eng, engine, key, back, run_up, extra, step):
            def turns(it, n, first=False, last=False):
                steps = n * SLOTS + (extra if last else 0)
                before = max(back, 0) if first else 0
                beyond = steps - n * SLOTS - back if last else 0
                buckets = [None] * (before * GROUPS_BLOCK)
                if steps > before:
                    buckets += buckets_from(engine, key, (it * SLOTS - back + before) * GROUPS_BLOCK,
                                            (steps - before - beyond) * GROUPS_BLOCK)
                for k in range(steps):
                    on = min(k // SLOTS, n - 1)
                    step(it + on, k - on * SLOTS, last, buckets[k * GROUPS_BLOCK:(k + 1) * GROUPS_BLOCK])
            assert ITERS % 2 == 0
            for u in range(-run_up, 0):
                step(0, u, False, None)
            turns(0, 1, first=True)
            with eng.Fori(0, (ITERS - 2) // 2) as pair:
                turns(pair * 2 + 1, 2)
            turns(ITERS - 1, 1, last=True)

        block = ctx.enter_context(nc.Block())

        @block.sync
        def _(sp):
            for tile, name in weights:
                sp.dma_start(tile[:, :], a[name]).then_inc(weights_in, 16)
            sp.wait_ge(consts_dve, 1)
            sp.dma_start(x_n[:, 0:BUCKETS - 1, :],
                         a["x"][0:(BUCKETS - 1) * P, :].rearrange("(b p) f -> p b f", p=P)).then_inc(x_in, 16)
            sp.dma_start(x_n[0:LAST, BUCKETS - 1, :], a["x"][(BUCKETS - 1) * P:N_NODES, :]).then_inc(x_in, 16)
            for n, k in enumerate(("dst", "src")):
                if n:
                    sp.wait_ge(hi_ready, n)
                sp.dma_start(idx_all, a[k].rearrange("(p j) -> p j", p=P)).then_inc(idx_in, 16)
                sp.wait_ge(hi_ready, n + 1)
                sp.dma_start(bucket_rows[k].rearrange("(p j) -> p j", p=P),
                             hi_bf[n]).then_inc(hi_out, 16)
            sp.wait_ge(hi_out, 32)

            def hi_row(k, c):
                return bucket_rows[k][bass.ds(c * CHUNK, CHUNK)].partition_broadcast(BUCKETS)

            sp.wait_ge(tables_read, 1)
            for k in ("dst", "src"):
                other, attr, width, last = ("src", "edge_attr_13", 13, "edge_type_8") if k == "dst" else \
                    ("dst", "edge_attr_8", EDGE_D, "edge_weight")

                def load(c2, s):
                    c = c2 * 2 + s
                    sp.wait_ge(hi_used[s], chunk_turns(k, c2, s))
                    sp.nop(nofuse=True)
                    sp.dma_start(hi_in[s][0:BUCKETS, :], hi_row(k, c)).then_inc(keys_in[s], 16)
                    sp.wait_ge(where_ready[s], chunk_turns(k, c2, s))
                    sp.nop(nofuse=True)
                    for tile, name in ((key_in, k), (other_in, other), (last_in, last)):
                        src_ap = a[name][bass.ds(c * CHUNK, CHUNK)].rearrange("(p j) -> p j", p=P)
                        if name == "edge_weight":
                            src_ap = src_ap.bitcast(I32)
                        sp.dma_start(tile[:, s, :], src_ap).then_inc(keys_in[s], 16)
                    if k == "src":
                        sp.wait_ge(attr_copied[s], c2 + 1)
                        sp.nop(nofuse=True)
                    sp.dma_start(attr_in[:, s, 0:J * width],
                                 a[attr][bass.ds(c * CHUNK, CHUNK), :].rearrange("(p j) f -> p (j f)", p=P)
                                 ).then_inc(keys_in[s], 16)
                chunk_loop(sp, load)
            for s in range(2):
                sp.wait_ge(records_out[s], 16 * J * chunk_turns("src", (CHUNKS - 1 - s) // 2, s))

            for p in ALL:
                sp.wait_ge(table_ready, p + 1)
                if p in (L0A, L0B, L2A, L3):
                    tab, t_in = tables[p], h_n
                elif p == L1:
                    tab, t_in = tables[p], wide
                else:
                    tab, t_in = tables[p].rearrange("(n r) f -> n (r f)", r=RELS), wide
                sp.dma_start(tab.rearrange("(b p) f -> p b f", p=P), t_in[:, :, :]).then_inc(table_out, 16)
                key = "dst" if p in BY_DST else "src"
                rows = recs[key].rearrange("(n p t) f -> n p (t f)", p=P, t=T)

                def load(it, u, last):
                    if p in (L0A, L0B) and not (isinstance(it, int) and it == 0):
                        sp.wait_ge(*marked(p, it, u, SLOTS))
                    else:
                        sp.wait_ge(*read.done(p, it, u, SLOTS))
                    sp.nop(nofuse=True)
                    sp.dma_start(rec[key][:, u, :, :].rearrange("p t f -> p (t f)"),
                                 rows[bass.ds(it * SLOTS + u, 1)].rearrange("n p w -> p (n w)")
                                 ).then_inc(rec_in.of(u), 16)
                block_loop(sp, load)
            sp.wait_ge(out_ready, 1)
            sp.dma_start(out[0:(BUCKETS - 1) * P, :].rearrange("(b p) f -> p b f", p=P),
                         x_n[:, 0:BUCKETS - 1, :]).then_inc(out_done, 16)
            sp.dma_start(out[(BUCKETS - 1) * P:N_NODES, :], x_n[0:LAST, BUCKETS - 1, :]).then_inc(out_done, 16)
            sp.wait_ge(out_done, 32)

        @block.gpsimd
        def _(pool):
            pool.iota(iota_p[:, :], pattern=[[0, 1]], base=0, channel_multiplier=1,
                      allow_small_or_imprecise_dtypes=True)
            pool.iota(iota_f[:, :], pattern=[[1, P]], base=0, channel_multiplier=0,
                      allow_small_or_imprecise_dtypes=True)
            pool.iota(iota_g[:, :], pattern=[[1, GROUPS]], base=0, channel_multiplier=0,
                      allow_small_or_imprecise_dtypes=True)
            pool.drain().then_inc(consts_pool, 1)

            for k in ("dst", "src"):
                pool.wait_ge(pads_out[k], 16 * PAD_DMAS)
                def scatter(c2, s):
                    if k == "src":
                        pool.wait_ge(attr_copied[s], c2 + 2)
                        pool.nop(nofuse=True)
                    pool.wait_ge(where_ready[s], chunk_turns(k, c2, s) + 1)
                    pool.nop(nofuse=True)
                    for j in range(J):
                        pool.indirect_dma_start(
                            recs[k], bass.IndirectOffsetOnAxis(ap=where[:, s, j:j + 1], axis=0),
                            rec_out[:, s, j, 0:REC[k]], None).then_inc(records_out[s], 16)
                chunk_loop(pool, scatter)

            for p in ALL:
                pool.wait_ge(table_out, 16 * (p + 1))
                width = TABLE_W[p]
                key = "dst" if p in BY_DST else "src"
                column = (C_LAST if p == L2B else C_OTHER)[key]

                def gather(it, u, last):
                    pool.wait_ge(*rec_in.done(p, it, u))
                    pool.nop(nofuse=True)
                    for t in range(T):
                        pool.indirect_dma_start(
                            got[:, u, t, 0:width], None, tables[p],
                            bass.IndirectOffsetOnAxis(ap=rec[key][:, u, t, column:column + 1].bitcast(I32), axis=0),
                        ).then_inc(gathered[p].of(u), 16)
                block_loop(pool, gather)

        @block.scalar
        def _(act):
            act.wait_ge(pad_ready, 1)
            for n, k in enumerate(("dst", "src")):
                if n:
                    act.wait_ge(tables_read, 1)
                rows = recs[k].rearrange("(n p r) f -> n p (r f)", p=P, r=PAD_ROWS)
                for m in range(PAD_DMAS):
                    act.dma_start(rows[m], pad_rec[k]).then_inc(pads_out[k], 16)
            for s in range(2):
                act.sem_inc(attr_copied[s], 1)

            def copy(c2, s):
                act.wait_ge(keys_in[s], 80 * chunk_turns("src", c2, s))
                act.wait_ge(records_out[s], 16 * J * (chunk_turns("src", c2, s) - 1))
                act.activation(rec_out[:, s, :, 0:EDGE_D],
                               attr_in[:, s, 0:J * EDGE_D].rearrange("p (j f) -> p j f", j=J),
                               ACT.Copy).then_inc(attr_copied[s], 1)
            chunk_loop(act, copy)

            def node(n, k_rows):
                act.wait_ge(node_src, n + 1)
                src = {N_GRU0: node_in, N_GRU1: node_in, N_Y: node_in, N_UPD: node_in, N_UPD2: node_in,
                       N_ROOT1: node_in, N_REL1: wide, N_Z: node_in, N_ROOT2: node_in}[n]

                def bring(i, v):
                    act.activation(stage[v][:, :, 0:k_rows], src[:, bass.ds(i * NODE_TILES, NODE_TILES), 0:k_rows],
                                   ACT.Copy).then_inc(staged, 1)

                def step(i, v, last):
                    if not last:
                        bring(i + 1, 1 - v)
                    act.wait_ge(node_turned, i + (n * NODE_STEPS + 1))
                    act.activation(turned[v][0:k_rows, :], ps_turn[0:k_rows, 0:NODE_TILES * P],
                                   ACT.Copy).then_inc(turned_ready, 1)
                    if n == N_UPD:
                        act.wait_ge(lin_done, i + 1)
                        act.activation(lin_t, ps_out[0][0:D, 0:NODE_TILES * P], ACT.Copy,
                                       scale=NORM_LIN).then_inc(lin_ready, 1)
                bring(0, 0)
                node_loop(act, step)

            n_to = [0]

            def unary(dst, src, func, scale=1.0, bias=0.0):
                n_to[0] += 1
                act.wait_ge(to_act, n_to[0])
                act.activation(dst, src, func, scale=scale, bias=bias).then_inc(from_act, 1)

            def root():
                unary(stat[:, 2, :], stat[:, 1, :], ACT.Sqrt)

            def l0_pass(p):
                act.wait_ge(pass_open, p + 1)

                def step(it, u, last):
                    if at := ahead(it, u, 1, last):
                        act.wait_ge(*hid_turned.done(p, *at))
                        act.activation(hid_t[:, at[1] % 2, :], ps_turn_bf[0:HID_W, :],
                                       ACT.Copy).then_inc(hid_ready.of(at[1]), 1)
                    if at := ahead(it, u, 3, last):
                        act.wait_ge(*attr_turned.done(p, *at))
                        act.activation(attr_t[:, at[1] % 2, :], ps_attr_bf[0:ATTR_W, :],
                                       ACT.Copy).then_inc(attr_ready.of(at[1]), 1)
                    if at := ahead(it, u, 2, last):
                        v = at[1] % 2
                        act.wait_ge(*marked(p, it, u))
                        act.activation(hid_parts[:, v, :, HID:2 * HID], hid_rest[:, v, :, :],
                                       ACT.Copy).then_inc(mid_ready.of(at[1]), 1)
                    if at := ahead(it, u, 1, last):
                        if old := ahead(it, u, -3, last):
                            act.wait_ge(*scattered.done(p, *old))
                        act.wait_ge(*rec_in.done(p, *at))
                        for t in range(T):
                            act.activation(onehot_bf[:, at[1], t, :], iota_f[:, :], ACT.Square, scale=-1.0,
                                           bias=rec["dst"][:, at[1], t, C_LANE["dst"]:C_LANE["dst"] + 1])
                        act.drain()
                        act.activation(onehot_bf[:, at[1], :, :], onehot_bf[:, at[1], :, :], ACT.Relu,
                                       scale=-1.0, bias=1.0).then_inc(oh_made.of(at[1]), 1)
                    if at := ahead(it, u, 3, last):
                        v = at[1] % 2
                        act.wait_ge(*hid_done.done(p, *at))
                        act.activation(hid[:, v, :, :], ps_hid, ACT.Relu)
                        act.activation(hid_parts[:, v, :, 0:HID], ps_hid, ACT.Relu).then_inc(relu_ready.of(at[1]), 1)
                for u in range(-3, 0):
                    step(0, u, False)
                block_loop(act, step)

            act.wait_ge(weights_in, 16 * len(weights))
            root()
            for p, n in ((L0A, N_GRU0), (L0B, N_GRU1)):
                l0_pass(p)
                node(n, 2 * D + 2)
                unary(gates[:, :, 0:2 * D], gates[:, :, 0:2 * D], ACT.Sigmoid)
                unary(t_n[:, :, :], t_n[:, :, :], ACT.Tanh)
            root()
            node(N_Y, D)
            act.wait_ge(pass_open, L1 + 1)

            def silu(it, u, last):
                act.wait_ge(*read.done(L1, it, u))
                act.wait_ge(*scattered.done(L1, it, u, 2))
                act.activation(msg16[:, u % 2, :, :], small[:, u % 2, :, :], ACT.Silu,
                               scale=NORM_MSG).then_inc(silu_ready.of(u), 1)
            for u in range(SLOTS):
                act.sem_inc(silu_ready.of(u), 1)
            block_loop(act, silu)
            node(N_UPD, D)
            unary(node_in[:, :, 0:D], t_n[:, :, :], ACT.Silu, scale=NORM_UPD)
            node(N_UPD2, D)
            root()
            node(N_ROOT1, D + 1)
            node(N_REL1, P)
            node(N_Z, HID)
            node(N_ROOT2, HID + 1)
            root()
            act.wait_ge(pass_open, L3 + 1)

            def step(it, u, last):
                if at := ahead(it, u, 2, last):
                    act.wait_ge(*oh_turned.done(L3, *at))
                    act.activation(onehot_t[:, at[1] % 2, :], ps_oht[:, :], ACT.Copy).then_inc(oht_ready.of(at[1]), 1)
            for u in range(-2, 0):
                step(0, u, False)
            block_loop(act, step)

        @block.vector
        def _(dve):
            dve.memset(x_n[:, BUCKETS - 1, :], 0.0)
            dve.memset(hid_parts[:, :, :, PARTS * HID:HID_W], 1.0)
            dve.memset(ones[:, :], 1.0)
            for k in ("dst", "src"):
                dve.memset(pad_rec[k], 0.0)
            dve.memset(rec_out[:, :, :, :], 0.0)
            dve.memset(msg_parts[:, :, :, :, D:D + 1], 0.0)
            dve.memset(agg17[:, :, :], 0.0)
            dve.drain()
            for k in ("dst", "src"):
                lane = C_LANE[k]
                dve.memset(pad_rec[k].rearrange("p (r f) -> p r f", f=REC[k])[:, :, lane:lane + 1], PAD_LANE)
            dve.memset(msg_parts[:, :, 0, :, D:D + 1], 1.0)
            dve.memset(rec_out[:, :, :, 0:ATTR_W // 2].bitcast(BF16)[:, :, :, ATTR_W - 1:ATTR_W], 1.0)
            dve.wait_ge(consts_pool, 1)
            dve.tensor_scalar(ident[:, :], iota_f[:, :], iota_p[:, 0:1], None, ALU.is_equal)
            dve.tensor_scalar(ident_bf[:, :], iota_f[:, :], iota_p[:, 0:1], None, ALU.is_equal)
            dve.tensor_scalar(upto[:, :], iota_f[:, :], iota_p[:, 0:1], None, ALU.is_ge)
            dve.drain().then_inc(consts_dve, 1)
            dve.drain().then_inc(pad_ready, 1)

            def bucket_rows_of(n):
                dve.wait_ge(idx_in, 16 * (n + 1))
                dve.tensor_scalar(hi_int, idx_all, 7, None, ALU.logical_shift_right)
                dve.drain()
                dve.tensor_copy(hi_bf[n], hi_int)
                dve.drain().then_inc(hi_ready, 1)
            bucket_rows_of(0)

            def count(b, buckets, found):
                dve.tensor_scalar(found, buckets, iota_f[:, bass.ds(b, 1)], None, ALU.is_equal, ALU.add,
                                  accum_out=counts[:, bass.ds(b, 1)])
                dve.drain()

            def tables_of(n, k):
                ng = n_groups[k][0:BUCKETS, :]
                dve.drain().then_inc(counts_ready, 1)
                dve.wait_ge(totals_ready, n + 1)
                dve.tensor_copy(ng, ps_total[0:BUCKETS, :])
                dve.drain()
                dve.tensor_scalar(n_i[0:BUCKETS, :], ng, float(GROUP - 1), None, ALU.add)
                dve.drain()
                dve.tensor_scalar(n_i[0:BUCKETS, :], n_i[0:BUCKETS, :], GROUP.bit_length() - 1, None,
                                  ALU.logical_shift_right)
                dve.drain()
                dve.tensor_copy(ng, n_i[0:BUCKETS, :])
                dve.drain().then_inc(n_groups_ready, 1)
                dve.wait_ge(ends_ready, n + 1)
                dve.tensor_copy(end_g[0:BUCKETS, :], ps_end[0:BUCKETS, :])
                dve.drain()
                dve.tensor_scalar(carry[k][0:BUCKETS, :], end_g[0:BUCKETS, :], ng, float(GROUP),
                                  ALU.subtract, ALU.mult)
                dve.tensor_scalar(started[0:BUCKETS, :], iota_g[0:BUCKETS, :], end_g[0:BUCKETS, 0:1], None,
                                  ALU.is_ge)
                dve.drain().then_inc(started_ready, 1)
                dve.wait_ge(bucket_ready, n + 1)
                dve.tensor_scalar(bucket_of[k][:, :], ps_bucket[0:1, 0:GROUPS], float(BUCKETS - 1), None, ALU.min)
                dve.drain().then_inc(tables_read, 1)

            with dve.Fori(0, BUCKETS) as b:
                count(b, hi_bf[0], eq[:, 0:N_EDGES // P])
            bucket_rows_of(1)
            tables_of(0, "dst")

            for s in range(2):
                dve.sem_inc(hi_used[s], 1)
                dve.sem_inc(where_ready[s], 1)
            for k in ("dst", "src"):
                if k == "src":
                    tables_of(1, "src")

                def place(c2, s):
                    dve.wait_ge(keys_in[s], 80 * chunk_turns(k, c2, s))
                    dve.tensor_scalar(eq[0:BUCKETS, :], hi_in[s][0:BUCKETS, :], iota_p[0:BUCKETS, 0:1], None,
                                      ALU.is_equal)
                    dve.drain().then_inc(hi_used[s], 1)
                    dve.tensor_tensor_scan(cum[0:BUCKETS, :], eq[0:BUCKETS, :], eq[0:BUCKETS, :],
                                           carry[k][0:BUCKETS, 0:1], ALU.add, ALU.max)
                    dve.drain()
                    dve.tensor_copy(carry[k][0:BUCKETS, :], cum[0:BUCKETS, CHUNK - 1:CHUNK])
                    dve.scalar_tensor_tensor(picked[s][0:BUCKETS, :], cum[0:BUCKETS, :], -1.0, eq[0:BUCKETS, :],
                                             ALU.add, ALU.mult)
                    dve.tensor_scalar(lane_i[:, :], key_in[:, s, :], P - 1, None, ALU.bitwise_and)
                    dve.drain().then_inc(picked_ready[s], 1)
                    if not (k == "dst" and isinstance(c2, int) and c2 == 0):
                        dve.wait_ge(records_out[s], 16 * J * (chunk_turns(k, c2, s) - 1))
                    out_i = rec_out[:, s, :, :].bitcast(I32)
                    dve.tensor_copy(rec_out[:, s, :, C_LANE[k]], lane_i[:, :])
                    dve.tensor_copy(out_i[:, :, C_OTHER[k]], other_in[:, s, :])
                    if k == "dst":
                        dve.tensor_scalar(pos_b[:, :], other_in[:, s, :], 3, None, ALU.logical_shift_left)
                        attr = attr_in[:, s, :].rearrange("p (j f) -> p j f", j=J)
                        parts = rec_out[:, s, :, 0:ATTR_W // 2].bitcast(BF16)
                        dve.tensor_copy(parts[:, :, 0:ATTR_D], attr)
                        dve.drain()
                        dve.tensor_tensor(out_i[:, :, C_LAST[k]], pos_b[:, :], last_in[:, s, :], ALU.bitwise_or)
                        dve.tensor_tensor(attr_rest[:, :, :], attr, parts[:, :, 0:ATTR_D], ALU.subtract)
                        dve.drain()
                        dve.tensor_copy(parts[:, :, ATTR_D:2 * ATTR_D], attr_rest[:, :, :])
                        dve.drain()
                        dve.tensor_tensor(parts[:, :, 2 * ATTR_D:3 * ATTR_D], attr_rest[:, :, :],
                                          parts[:, :, ATTR_D:2 * ATTR_D], ALU.subtract)
                    else:
                        dve.tensor_copy(out_i[:, :, C_LAST[k]], last_in[:, s, :])
                    if k == "dst":
                        for n in range(COUNTS_CHUNK):
                            count((c2 * 2 + s) * COUNTS_CHUNK + n, hi_bf[1], src_eq)
                    dve.wait_ge(pos_ready[s], chunk_turns(k, c2, s))
                    dve.tensor_copy(pos_i[:, :], ps_pos[s][:, :])
                    dve.drain()
                    dve.tensor_scalar(pos_b[:, :], pos_i[:, :], GROUP - TILES_GROUP, 1, ALU.bitwise_and,
                                      ALU.logical_shift_left)
                    dve.tensor_scalar(pos_c[:, :], pos_i[:, :], GROUP, 7, ALU.bitwise_and,
                                      ALU.logical_shift_right)
                    dve.tensor_scalar(pos_i[:, :], pos_i[:, :], (1 << 24) - BLOCK + 1, None, ALU.bitwise_and)
                    dve.drain()
                    dve.tensor_tensor(pos_b[:, :], pos_b[:, :], pos_c[:, :], ALU.bitwise_or)
                    dve.drain()
                    dve.tensor_tensor(where[:, s, :], pos_b[:, :], pos_i[:, :], ALU.bitwise_or)
                    dve.drain().then_inc(where_ready[s], 1)
                chunk_loop(dve, place)

            n_act = [0]

            def through_act():
                n_act[0] += 1
                dve.drain().then_inc(to_act, 1)
                dve.wait_ge(from_act, n_act[0])

            def per_node(v):
                return v.unsqueeze(2).to_broadcast([P, BUCKETS, D])

            def layernorm_relu():
                dve.tensor_reduce(stat[:, 0, :], x_n[:, :, :], AX.X, ALU.add)
                dve.drain()
                dve.tensor_scalar(stat[:, 0, :], stat[:, 0, :], 1.0 / D, None, ALU.mult)
                dve.drain()
                dve.tensor_tensor(h_n[:, :, :], x_n[:, :, :], per_node(stat[:, 0, :]), ALU.subtract)
                dve.drain()
                dve.tensor_tensor(t_n[:, :, :], h_n[:, :, :], h_n[:, :, :], ALU.mult)
                dve.drain()
                dve.tensor_reduce(stat[:, 1, :], t_n[:, :, :], AX.X, ALU.add)
                dve.drain()
                dve.tensor_scalar(stat[:, 1, :], stat[:, 1, :], 1.0 / D, LN_EPS, ALU.mult, ALU.add)
                through_act()
                dve.reciprocal(stat[:, 2, :], stat[:, 2, :])
                dve.drain()
                dve.tensor_tensor(h_n[:, :, :], h_n[:, :, :], per_node(stat[:, 2, :]), ALU.mult)
                dve.drain()
                dve.tensor_scalar(h_n[:, :, :], h_n[:, :, :], 0.0, None, ALU.max)
                dve.drain()

            def node(n, consume):
                dve.drain().then_inc(node_src, 1)

                def step(i, v, last):
                    dve.wait_ge(node_out, i + (n * NODE_STEPS + 1))
                    consume(bass.ds(i * NODE_TILES, NODE_TILES), v)
                    dve.drain().then_inc(node_used, 1)
                node_loop(dve, step)

            def product(v, width):
                return ps_out[v][:, 0:NODE_TILES * width].rearrange("p (t f) -> p t f", t=NODE_TILES)

            def make_onehot(key, u):
                v = u % 2
                dve.tensor_tensor(onehot[:, v, :, :], iota_f[:, :].unsqueeze(1).to_broadcast([P, T, P]),
                                  rec[key][:, u, :, C_LANE[key]:C_LANE[key] + 1].to_broadcast([P, T, P]), ALU.is_equal)

            def turn_buckets(p, it, first=0):
                key = "dst" if p in BY_DST else "src"
                return [None] * (first * GROUPS_BLOCK) + buckets_from(
                    mybir.EngineType.DVE, key, (it * SLOTS - 1 + first) * GROUPS_BLOCK, (SLOTS - first) * GROUPS_BLOCK)

            def add_group(it, u, back, g, bucket, sums, width):
                to = sums[:, bass.ds(bucket, 1), :].rearrange("p b f -> p (b f)")
                dve.tensor_tensor(to, to, acc((u - back) % 2, width)[:, g, :], ALU.add)

            def add_sums(p, it, u, buckets, sums, width):
                dve.wait_ge(*scattered.done(p, it, u, 1))
                for g in range(GROUPS_BLOCK):
                    add_group(it, u, 1, g, buckets[u * GROUPS_BLOCK + g], sums, width)
                    done = dve.drain()
                done.then_inc(added.of((u - 1) % SLOTS), 1)

            def edge_loop(p, step, sums, width):
                dve.drain().then_inc(pass_open, 1)

                def turn(it, last, first=0):
                    buckets = turn_buckets(p, it, first)
                    for u in range(SLOTS):
                        step(it, u, last, lambda: u < first or add_sums(p, it, u, buckets, sums, width))
                turn(0, False, 1)
                with dve.Fori(1, ITERS - 1) as it:
                    turn(it, False)
                turn(ITERS - 1, True)
                buckets = buckets_from(mybir.EngineType.DVE, "dst" if p in BY_DST else "src",
                                       GROUPS - GROUPS_BLOCK, GROUPS_BLOCK)
                add_sums(p, ITERS, 0, buckets, sums, width)

            for u in range(SLOTS):
                for s in (read, added):
                    dve.sem_inc(s.of(u), 1)
            dve.sem_inc(node_used, 2)

            dve.wait_ge(weights_in, 16 * len(weights))
            for w, parts in ((w1, w1_parts), (w2, w2_parts)):
                for n in range(PARTS):
                    dve.tensor_copy(parts[:, n, :], w[:, :])
                    dve.drain()
                    if n < PARTS - 1:
                        dve.tensor_tensor(w[:, :], w[:, :], parts[:, n, :], ALU.subtract)
                        dve.drain()
            dve.wait_ge(x_in, 32)
            layernorm_relu()
            dve.drain().then_inc(table_ready, 1)
            dve.memset(node_in[:, :, 2 * D:2 * D + 2], 1.0)
            agg_of = [agg17, big[:, :, 0:D + 1]]
            for p, n in ((L0A, N_GRU0), (L0B, N_GRU1)):
                def step(it, u, last, buckets):
                    now, soon = ahead(it, u, 0, last), ahead(it, u, 2, last)
                    late, later, sums = ahead(it, u, -1, last), ahead(it, u, -2, last), ahead(it, u, -4, last)
                    v, v1 = u % 2, (u - 1) % 2
                    if sums:
                        dve.wait_ge(*scattered.done(p, *sums))
                        for g in range(GROUPS_BLOCK):
                            add_group(it, u, 4, g, buckets[g], agg_of[g], D + 1)
                    if late:
                        dve.tensor_copy(msg_parts[:, late[1], 0, :, 0:D], msg[:, v1, :, :])
                    if later:
                        dve.tensor_tensor(msg_parts[:, later[1], 2, :, 0:D], msg_rest[:, v, :, :],
                                          msg_parts[:, later[1], 1, :, 0:D], ALU.subtract)
                    if now:
                        dve.wait_ge(*gathered[p].done(p, *now))
                        dve.wait_ge(*w_done.done(p, *now))
                        dve.tensor_tensor(prod[:, :, :].rearrange("p t (i o) -> p t i o", i=D),
                                          ps_w[v].rearrange("p t (i o) -> p t i o", i=D),
                                          got[:, u, :, 0:D].unsqueeze(3).to_broadcast([P, T, D, D]), ALU.mult)
                    if soon:
                        vs = soon[1] % 2
                        dve.wait_ge(*relu_ready.done(p, *soon))
                        dve.tensor_tensor(hid_rest[:, vs, :, :], hid[:, vs, :, :], hid_parts[:, vs, :, 0:HID],
                                          ALU.subtract)
                    dve.drain().then_inc(step_mark, 1)
                    if late:
                        dve.tensor_tensor(msg_rest[:, v1, :, :], msg[:, v1, :, :], msg_parts[:, late[1], 0, :, 0:D],
                                          ALU.subtract)
                    if now:
                        dve.tensor_reduce(msg[:, v, :, :], prod[:, :, :].rearrange("p t (i o) -> p t o i", i=D),
                                          AX.X, ALU.add)
                    done = dve.drain()
                    if now:
                        done.then_inc(read.of(u), 1)
                    if late:
                        dve.tensor_copy(msg_parts[:, late[1], 1, :, 0:D], msg_rest[:, v1, :, :])
                    if soon:
                        dve.wait_ge(*mid_ready.done(p, *soon))
                        dve.tensor_tensor(hid_parts[:, vs, :, 2 * HID:3 * HID], hid_rest[:, vs, :, :],
                                          hid_parts[:, vs, :, HID:2 * HID], ALU.subtract)
                    done = dve.drain()
                    if soon:
                        done.then_inc(parts_ready.of(soon[1]), 1)

                dve.memset(agg_of[1], 0.0)
                dve.drain().then_inc(pass_open, 1)
                sweep(dve, mybir.EngineType.DVE, "dst", 4, 2, 4, step)
                dve.drain()
                dve.tensor_tensor(agg17[:, :, :], agg17[:, :, :], agg_of[1], ALU.add)
                dve.drain()
                dve.tensor_scalar(stat[:, 0, :], agg17[:, :, D], 1.0, None, ALU.max)
                dve.drain()
                dve.reciprocal(stat[:, 0, :], stat[:, 0, :])
                dve.drain()
                dve.tensor_tensor(node_in[:, :, 0:D], agg16, per_node(stat[:, 0, :]), ALU.mult)
                dve.tensor_copy(node_in[:, :, D:2 * D], h_n[:, :, :])
                node(n, lambda b, v: dve.tensor_copy(gates[:, b, :], product(v, 4 * D)))
                through_act()
                dve.tensor_tensor(t_n[:, :, :], gates[:, :, 0:D], gates[:, :, 3 * D:4 * D], ALU.mult)
                dve.drain()
                dve.tensor_tensor(t_n[:, :, :], t_n[:, :, :], gates[:, :, 2 * D:3 * D], ALU.add)
                through_act()
                dve.tensor_tensor(h_n[:, :, :], h_n[:, :, :], t_n[:, :, :], ALU.subtract)
                dve.drain()
                dve.tensor_tensor(h_n[:, :, :], h_n[:, :, :], gates[:, :, D:2 * D], ALU.mult)
                dve.drain()
                dve.tensor_tensor(h_n[:, :, :], h_n[:, :, :], t_n[:, :, :], ALU.add)
                dve.memset(agg17[:, :, :], 0.0)
                dve.drain()
                if p == L0A:
                    dve.drain().then_inc(table_ready, 1)
            dve.tensor_tensor(x_n[:, :, :], x_n[:, :, :], h_n[:, :, :], ALU.add)
            dve.drain()

            layernorm_relu()
            dve.tensor_copy(node_in[:, :, 0:D], h_n[:, :, :])
            node(N_Y, lambda b, v: dve.tensor_copy(wide[:, b, :], product(v, P)))
            dve.drain().then_inc(table_ready, 1)

            def step(it, u, last, add):
                v = u % 2
                dve.wait_ge(*scattered.done(L1, it, u, 2))
                dve.wait_ge(*rec_in.done(L1, it, u))
                make_onehot("src", u)
                dve.wait_ge(*gathered[L1].done(L1, it, u))
                pv = prod[:, :, 0:D * EDGE_D].rearrange("p t (h j) -> p t h j", h=D)
                dve.tensor_tensor(pv, got[:, u, :, :].rearrange("p t (h j) -> p t h j", h=D),
                                  rec["src"][:, u, :, 0:EDGE_D].unsqueeze(2).to_broadcast([P, T, D, EDGE_D]), ALU.mult)
                dve.drain()
                dve.wait_ge(*silu_ready.done(L1, it, u, 2))
                dve.tensor_reduce(small[:, v, :, :], pv, AX.X, ALU.add)
                dve.drain().then_inc(read.of(u), 1)
                add()
            edge_loop(L1, step, agg16, D)
            dve.tensor_copy(node_in[:, :, 0:D], agg16)
            dve.drain()
            dve.memset(agg17[:, :, :], 0.0)

            def bilinear(b, _):
                v = ps_v[:, 0:NODE_TILES * D * D].rearrange("p (t k i) -> p t k i", t=NODE_TILES, k=D)
                big_flat = big[:, :, :].rearrange("p b f -> p (b f)")[:, 0:NODE_TILES * D * D]
                big_flat = big_flat.rearrange("p (t k i) -> p t k i", t=NODE_TILES, k=D)
                dve.tensor_tensor(big_flat, v, h_n[:, b, :].unsqueeze(2).to_broadcast([P, NODE_TILES, D, D]),
                                  ALU.mult)
                dve.drain()
                dve.tensor_reduce(t_n[:, b, :], big_flat, AX.X, ALU.add)
            node(N_UPD, bilinear)
            through_act()
            node(N_UPD2, lambda b, v: dve.tensor_scalar(t_n[:, b, :], product(v, D), NORM_LIN, None, ALU.mult))
            dve.tensor_tensor(t_n[:, :, :], t_n[:, :, :], h_n[:, :, :], ALU.add)
            dve.drain()
            dve.tensor_tensor(x_n[:, :, :], x_n[:, :, :], t_n[:, :, :], ALU.add)
            dve.drain()

            layernorm_relu()
            dve.drain().then_inc(table_ready, 1)
            dve.tensor_copy(node_in[:, :, 0:D], h_n[:, :, :])
            dve.memset(node_in[:, :, D:D + 1], 1.0)
            root_part = gates[:, :, 0:HID]
            node(N_ROOT1, lambda b, v: dve.tensor_copy(gates[:, b, 0:HID], product(v, HID)))
            dve.memset(big[:, :, :], 0.0)

            for p in (L2A, L2B):
                width = W2A if p == L2A else RELS * D

                def step(it, u, last, add):
                    v = u % 2
                    dve.wait_ge(*scattered.done(p, it, u, 2))
                    dve.wait_ge(*rec_in.done(p, it, u))
                    make_onehot("dst", u)
                    dve.tensor_scalar(rel_i[:, :], rec["dst"][:, u, :, C_LAST["dst"]].bitcast(I32), RELS - 1, None,
                                      ALU.bitwise_and)
                    dve.drain()
                    mask = msgw[:, v, :, RELS * D:W2A]
                    dve.tensor_tensor(mask, iota_f[:, 0:RELS].unsqueeze(1).to_broadcast([P, T, RELS]),
                                      rel_i[:, :].unsqueeze(2).to_broadcast([P, T, RELS]), ALU.is_equal)
                    dve.drain()
                    dve.wait_ge(*gathered[p].done(p, it, u))
                    dve.tensor_tensor(msgw[:, v, :, 0:RELS * D].rearrange("p t (r f) -> p t r f", r=RELS),
                                      mask.unsqueeze(3).to_broadcast([P, T, RELS, D]),
                                      got[:, u, :, 0:D].unsqueeze(2).to_broadcast([P, T, RELS, D]), ALU.mult)
                    dve.drain().then_inc(read.of(u), 1)
                    add()
                edge_loop(p, step, big[:, :, 0:width], width)
                if p == L2A:
                    dve.tensor_scalar(inv[:, :, :], big[:, :, RELS * D:W2A], 1.0, None, ALU.max)
                    dve.drain()
                    dve.reciprocal(inv[:, :, :], inv[:, :, :])
                    dve.drain()
                for r in range(RELS):
                    part = big[:, :, r * D:(r + 1) * D]
                    dve.tensor_tensor(part, part, inv[:, :, r:r + 1].to_broadcast([P, BUCKETS, D]), ALU.mult)
                if p == L2A:
                    node(N_REL1, lambda b, v: dve.tensor_tensor(gates[:, b, 0:HID], product(v, HID), gates[:, b, 0:HID],
                                                             ALU.add))
                    dve.tensor_scalar(node_in[:, :, 0:HID], root_part, 0.0, None, ALU.max)
                    dve.memset(node_in[:, :, HID:HID + 1], 1.0)
                    node(N_Z, lambda b, v: dve.tensor_copy(wide[:, b, :], product(v, P)))
                    dve.drain().then_inc(table_ready, 1)
                    node(N_ROOT2, lambda b, v: dve.tensor_copy(t_n[:, b, :], product(v, D)))
                    dve.wait_ge(table_out, 16 * (L2B + 1))
                    dve.memset(big[:, :, 0:RELS * D], 0.0)
            dve.drain()
            dve.tensor_reduce(u_n[:, :, :], big[:, :, 0:RELS * D].rearrange("p b (r f) -> p b f r", r=RELS),
                              AX.X, ALU.add)
            dve.drain()
            dve.tensor_tensor(t_n[:, :, :], t_n[:, :, :], u_n[:, :, :], ALU.add)
            dve.drain()
            dve.tensor_tensor(x_n[:, :, :], x_n[:, :, :], t_n[:, :, :], ALU.add)
            dve.drain()

            layernorm_relu()
            dve.drain().then_inc(table_ready, 1)
            dve.memset(agg_of[1][:, :, 0:D], 0.0)
            dve.drain().then_inc(pass_open, 1)

            def uptake(it, u, last, buckets):
                now, soon, sums = ahead(it, u, 0, last), ahead(it, u, 2, last), ahead(it, u, -2, last)
                v = u % 2
                den, num = small[:, 0, :, :], small[:, 1, :, :]
                if sums:
                    dve.wait_ge(*scattered.done(L3, *sums))
                    for g in range(GROUPS_BLOCK):
                        add_group(it, u, 2, g, buckets[g], agg_of[g][:, :, 0:D], D)
                if soon:
                    dve.wait_ge(*rec_in.done(L3, *soon))
                    dve.tensor_tensor(onehot4[:, soon[1], :, :], iota_f[:, :].unsqueeze(1).to_broadcast([P, T, P]),
                                      rec["src"][:, soon[1], :, C_LANE["src"]:C_LANE["src"] + 1]
                                      .to_broadcast([P, T, P]), ALU.is_equal)
                if now:
                    xj = got[:, u, :, 0:D]
                    dve.wait_ge(*gathered[L3].done(L3, it, u))
                    dve.tensor_scalar(den, xj, 0.1, 5.0, ALU.mult, ALU.add)
                    dve.tensor_tensor(num, xj, rec["src"][:, u, :, C_LAST["src"]:C_LAST["src"] + 1]
                                      .to_broadcast([P, T, D]), ALU.mult)
                done = dve.drain()
                if soon:
                    done.then_inc(oh_ready.of(soon[1]), 1)
                if not now:
                    return
                dve.wait_ge(*xi_done.done(L3, it, u))
                dve.scalar_tensor_tensor(den, ps_xi[v], 0.9, den, ALU.mult, ALU.add)
                dve.tensor_tensor(num, num, ps_xi[v], ALU.mult)
                dve.drain()
                dve.reciprocal(den, den)
                dve.drain()
                dve.tensor_tensor(msg16[:, v, :, :], num, den, ALU.mult)
                dve.drain().then_inc(read.of(u), 1)
            sweep(dve, mybir.EngineType.DVE, "src", 2, 2, 2, uptake)
            dve.tensor_tensor(agg16, agg16, agg_of[1][:, :, 0:D], ALU.add)
            dve.drain()
            dve.tensor_scalar(t_n[:, :, :], h_n[:, :, :], -1.0 / 5.0, 1.0, ALU.mult, ALU.add)
            dve.tensor_scalar(u_n[:, :, :], h_n[:, :, :], 1.0, None, ALU.subtract)
            dve.drain()
            dve.tensor_tensor(t_n[:, :, :], t_n[:, :, :], h_n[:, :, :], ALU.mult)
            dve.drain()
            dve.tensor_tensor(t_n[:, :, :], t_n[:, :, :], u_n[:, :, :], ALU.mult)
            dve.drain()
            dve.scalar_tensor_tensor(t_n[:, :, :], t_n[:, :, :], 0.1, agg16, ALU.add, ALU.add)
            dve.drain()
            dve.tensor_tensor(x_n[:, :, :], x_n[:, :, :], t_n[:, :, :], ALU.add)
            dve.drain().then_inc(out_ready, 1)

        @block.tensor
        def _(pe):
            pe.wait_ge(consts_dve, 1)
            for n, k in enumerate(("dst", "src")):
                pe.wait_ge(counts_ready, n + 1)
                pe.matmul(ps_total[0:BUCKETS, :], counts[:, 0:BUCKETS], ones[:, 0:1],
                          start=True, stop=True).then_inc(totals_ready, 1)
                pe.wait_ge(n_groups_ready, n + 1)
                pe.matmul(ps_end[0:BUCKETS, :], upto[0:BUCKETS, 0:BUCKETS],
                          n_groups[k][0:BUCKETS, :], start=True, stop=True).then_inc(ends_ready, 1)
                pe.wait_ge(started_ready, n + 1)
                for c in range(0, GROUPS, BANK):
                    e = min(c + BANK, GROUPS)
                    last = pe.matmul(ps_bucket[0:1, c:e], ones[0:BUCKETS, 0:1], started[0:BUCKETS, c:e],
                                     start=True, stop=True)
                last.then_inc(bucket_ready, 1)

                def collect(c2, s):
                    pe.wait_ge(picked_ready[s], chunk_turns(k, c2, s))
                    pe.wait_ge(where_ready[s], chunk_turns(k, c2, s))
                    cells = picked[s][0:BUCKETS, :].rearrange("b (p j) -> b j p", j=J)
                    for j in range(J):
                        last = pe.matmul(ps_pos[s][:, j:j + 1], cells[:, j, :], ones[0:BUCKETS, 0:1],
                                         start=True, stop=True)
                    last.then_inc(pos_ready[s], 1)
                chunk_loop(pe, collect)

            def scatter(p, it, u, rhs, width, ready):
                v = u % 2
                pe.wait_ge(*ready.done(p, it, u))
                pe.wait_ge(*added.done(p, it, u, 2))
                for g in range(GROUPS_BLOCK):
                    for t in range(TILES_GROUP):
                        tt = g * TILES_GROUP + t
                        last = pe.matmul(acc(v, width)[:, g, :], onehot[:, v, tt, :], rhs[:, v, tt, 0:width],
                                         start=(t == 0), stop=(t == TILES_GROUP - 1))
                last.then_inc(scattered.of(u), 1)

            def node(n, k_rows, w, width):
                def turn(i, v):
                    pe.wait_ge(staged, i + (n * NODE_STEPS + 1))
                    pe.nop(nofuse=True)
                    for t in range(NODE_TILES):
                        end = pe.transpose(ps_turn[0:k_rows, t * P:(t + 1) * P], stage[v][:, t, 0:k_rows], ident[:, :])
                    end.then_inc(node_turned, 1)

                def step(i, v, last):
                    pe.wait_ge(turned_ready, i + (n * NODE_STEPS + 1))
                    pe.nop(nofuse=True)
                    if not last:
                        turn(i + 1, 1 - v)
                    if n == N_UPD:
                        for c in range(0, NODE_TILES * P, BANK):
                            e = min(c + BANK, NODE_TILES * P)
                            end = pe.matmul(ps_out[0][0:D, c:e], wlin[:, :], turned[v][0:D, c:e],
                                            start=True, stop=True)
                        end.then_inc(lin_done, 1)
                        pe.wait_ge(lin_ready, i + 1)
                        pe.wait_ge(node_used, i + (n * NODE_STEPS + 2))
                    else:
                        pe.wait_ge(node_used, i + (n * NODE_STEPS + 1))
                    pe.nop(nofuse=True)
                    for t in range(NODE_TILES):
                        if n == N_UPD:
                            to, lhs = ps_v[:, t * D * D:(t + 1) * D * D], lin_t[:, t * P:(t + 1) * P]
                        else:
                            to, lhs = ps_out[v][:, t * width:(t + 1) * width], turned[v][0:k_rows, t * P:(t + 1) * P]
                        end = pe.matmul(to, lhs, w[:, :], start=True, stop=True)
                    end.then_inc(node_out, 1)
                turn(0, 0)
                node_loop(pe, step)

            for u in range(SLOTS):
                pe.sem_inc(scattered.of(u), 1)
            pe.wait_ge(weights_in, 16 * len(weights))

            def matrices(v, tiles):
                for t in tiles:
                    for n in range(PARTS):
                        end = pe.matmul(ps_w[v][:, t, :], hid_t[:, v, t * P:(t + 1) * P],
                                        w2_parts[:, n, :], start=(n == 0), stop=(n == PARTS - 1))
                return end

            for p, n in ((L0A, N_GRU0), (L0B, N_GRU1)):
                def step(it, u, last):
                    soon, later, back = ahead(it, u, 1, last), ahead(it, u, 3, last), ahead(it, u, -3, last)
                    if soon:
                        vs = soon[1] % 2
                        pe.wait_ge(*parts_ready.done(p, *soon))
                        pe.nop(nofuse=True)
                        for t in range(T):
                            end = pe.transpose(ps_turn_bf[0:HID_W, t * P:(t + 1) * P],
                                               hid_parts[:, vs, t, 0:HID_W], ident_bf[:, :])
                        end.then_inc(hid_turned.of(soon[1]), 1)
                    if back:
                        v = back[1] % 2
                        pe.wait_ge(*marked(p, it, u, 1))
                        pe.wait_ge(*oh_made.done(p, *back))
                        pe.nop(nofuse=True)
                        for g in range(GROUPS_BLOCK):
                            for t in range(g * TILES_GROUP, (g + 1) * TILES_GROUP):
                                for n in range(PARTS):
                                    end = pe.matmul(acc(v, D + 1)[:, g, :], onehot_bf[:, back[1], t, :],
                                                    msg_parts[:, back[1], n, t, :],
                                                    start=(t == g * TILES_GROUP and n == 0),
                                                    stop=(t == (g + 1) * TILES_GROUP - 1 and n == PARTS - 1))
                        end.then_inc(scattered.of(back[1]), 1)
                    if later:
                        if before := ahead(it, u, 2, last):
                            pe.wait_ge(*relu_ready.done(p, *before))
                        pe.wait_ge(*rec_in.done(p, *later))
                        pe.nop(nofuse=True)
                        for t in range(T):
                            attr = rec["dst"][:, later[1], t, 0:ATTR_W // 2].bitcast(BF16)
                            end = pe.transpose(ps_attr_bf[0:ATTR_W, t * P:(t + 1) * P], attr, ident_bf[:, :])
                        end.then_inc(attr_turned.of(later[1]), 1)
                    if soon:
                        pe.wait_ge(*hid_ready.done(p, *soon))
                        pe.wait_ge(*read.done(p, *soon, 2))
                        pe.nop(nofuse=True)
                        matrices(vs, range(T // 2))
                    if later:
                        pe.wait_ge(*attr_ready.done(p, *later))
                        pe.nop(nofuse=True)
                        for t in range(T):
                            for n in range(PARTS):
                                end = pe.matmul(ps_hid[:, t, :], attr_t[:, later[1] % 2, t * P:(t + 1) * P],
                                                w1_parts[:, n, :], start=(n == 0), stop=(n == PARTS - 1))
                        end.then_inc(hid_done.of(later[1]), 1)
                    if soon:
                        matrices(vs, range(T // 2, T)).then_inc(w_done.of(soon[1]), 1)
                pe.wait_ge(pass_open, p + 1)
                for u in range(-3, 0):
                    step(0, u, False)
                for u in range(SLOTS):
                    step(0, u, False)
                with pe.Fori(1, ITERS - 1) as it:
                    for u in range(SLOTS):
                        step(it, u, False)
                for u in range(SLOTS + 3):
                    step(ITERS - 1, u, True)
                node(n, 2 * D + 2, wg, 4 * D)
            node(N_Y, D, wy, P)
            pe.wait_ge(pass_open, L1 + 1)
            block_loop(pe, lambda it, u, last: scatter(L1, it, u, msg16, D, silu_ready))
            node(N_UPD, D, wupd, D * D)
            node(N_UPD2, D, wupd2, D)
            node(N_ROOT1, D + 1, wroot1, HID)
            pe.wait_ge(pass_open, L2A + 1)
            block_loop(pe, lambda it, u, last: scatter(L2A, it, u, msgw, W2A, read))
            node(N_REL1, P, wrel1, HID)
            node(N_Z, HID, wz, P)
            node(N_ROOT2, HID + 1, wroot2, D)
            pe.wait_ge(pass_open, L2B + 1)
            block_loop(pe, lambda it, u, last: scatter(L2B, it, u, msgw, RELS * D, read))
            pe.wait_ge(pass_open, L3 + 1)

            def step(it, u, last, buckets):
                later = ahead(it, u, 2, last)
                if at := ahead(it, u, 1, last):
                    v = at[1] % 2
                    if buckets is None:
                        buckets = buckets_from(mybir.EngineType.PE, "src", 0, GROUPS_BLOCK)
                    pe.wait_ge(*oht_ready.done(L3, *at))
                    pe.wait_ge(*read.done(L3, *at, 2))
                    for t in range(T):
                        end = pe.matmul(ps_xi[v][:, t, :], onehot_t[:, v, t * P:(t + 1) * P],
                                        h_n[:, bass.ds(buckets[t // TILES_GROUP], 1), :].rearrange("p b f -> p (b f)"),
                                        start=True, stop=True)
                    end.then_inc(xi_done.of(at[1]), 1)
                if later:
                    pe.wait_ge(*oh_ready.done(L3, *later))
                    pe.nop(nofuse=True)
                    for t in range(T):
                        end = pe.transpose(ps_oht[:, t * P:(t + 1) * P], onehot4_bf[:, later[1], t, :], ident_bf[:, :])
                    end.then_inc(oh_turned.of(later[1]), 1)
                if back := ahead(it, u, -1, last):
                    v = back[1] % 2
                    pe.wait_ge(*read.done(L3, *back))
                    pe.nop(nofuse=True)
                    for g in range(GROUPS_BLOCK):
                        for t in range(TILES_GROUP):
                            tt = g * TILES_GROUP + t
                            end = pe.matmul(acc(v, D)[:, g, :], onehot4[:, back[1], tt, :], msg16[:, v, tt, :],
                                            start=(t == 0), stop=(t == TILES_GROUP - 1))
                    end.then_inc(scattered.of(back[1]), 1)
            sweep(pe, mybir.EngineType.PE, "src", -1, 2, 1, step)


def kernel(**inputs):
    import numpy as _np
    import concourse.bacc as _bacc
    from concourse import mybir as _mybir
    from concourse.bass_utils import run_bass_kernel_spmd as _run

    i = {k: _np.ascontiguousarray(v) for k, v in inputs.items()}
    ih, hh = i["L0_gnn_gru_w_ih"], i["L0_gnn_gru_w_hh"]
    arrays = {k: i[k] for k in ("x", "src", "dst", "edge_attr_13", "edge_attr_8", "edge_type_8", "edge_weight")}
    arrays["w1"] = _np.concatenate([i["L0_gnn_fnet_w1"]] * PARTS + [i["L0_gnn_fnet_b1"][None, :]], 0)
    arrays["w2"] = _np.concatenate([i["L0_gnn_fnet_w2"]] * PARTS + [i["L0_gnn_fnet_b2"][None, :]], 0)
    wg = _np.zeros((2 * D + 2, 4 * D), _np.float32)
    wg[0:D, 0:3 * D] = ih.T
    wg[D:2 * D, 0:2 * D], wg[D:2 * D, 3 * D:] = hh.T[:, :2 * D], hh.T[:, 2 * D:]
    wg[2 * D, 0:3 * D] = i["L0_gnn_gru_b_ih"]
    wg[2 * D + 1, 0:2 * D], wg[2 * D + 1, 3 * D:] = i["L0_gnn_gru_b_hh"][:2 * D], i["L0_gnn_gru_b_hh"][2 * D:]
    arrays["wg"] = wg
    arrays["wy"] = _np.ascontiguousarray(i["L1_gnn_W_msg_tp"].transpose(0, 2, 1)).reshape(D, D * EDGE_D)
    arrays["wlin"] = i["L1_gnn_W_msg_lin"]
    arrays["wupd"] = _np.ascontiguousarray(i["L1_gnn_W_upd_tp"].transpose(1, 2, 0)).reshape(D, D * D)
    arrays["wupd2"] = i["L1_gnn_W_upd_lin"]
    arrays["wroot1"] = _np.concatenate([i["L2_gnn_root1"], i["L2_gnn_b1"][None, :]], 0)
    arrays["wrel1"] = i["L2_gnn_W1"].reshape(RELS * D, HID)
    arrays["wz"] = _np.ascontiguousarray(i["L2_gnn_W2"].transpose(1, 0, 2)).reshape(HID, RELS * D)
    arrays["wroot2"] = _np.concatenate([i["L2_gnn_root2"], i["L2_gnn_b2"][None, :]], 0)

    nc = _bacc.Bacc("TRN2", target_bir_lowering=False, num_devices=1)
    args = {k: nc.dram_tensor(f"in_{k}", v.shape, _mybir.dt.from_np(v.dtype), kind="ExternalInput").ap()
            for k, v in arrays.items()}
    out = nc.dram_tensor("out", (N_NODES, D), _mybir.dt.float32, kind="ExternalOutput").ap()
    gnn_kernel(nc, args, out)
    r = _run(nc, [{f"in_{k}": v for k, v in arrays.items()}], core_ids=[0])
    return r.results[0]["out"]
```
